# Optimizing a Trainium2 kernel written in Bass

```python
import numpy as np
import jax
import jax.numpy as jnp

def _softmax(x, axis=-1):
    return jax.nn.softmax(x, axis=axis)

def _gelu(x):
    return jax.nn.gelu(x, approximate=True)

def _silu(x):
    return jax.nn.silu(x)

def _sigmoid(x):
    return jax.nn.sigmoid(x)

def _layernorm(x, axis=-1, eps=1e-05):
    m = jnp.mean(x, axis=axis, keepdims=True)
    v = jnp.var(x, axis=axis, keepdims=True)
    return (x - m) / jnp.sqrt(v + eps)

def _scatter_add(tgt, idx, src, axis=0):
    return tgt.at[idx].add(src)

def _segment_sum(src, seg, n):
    return jax.ops.segment_sum(src, seg, n)
kernel_name = 'mk_prb_d1_jaxref_r4_805a1b'

def setup_inputs(seed: int=0):
    np.random.seed(seed)
    _w = jnp.asarray

    def _L0_attn_setup():
        import jax, jax.numpy as jnp
        import numpy as np
        E, H, W = (256, 16, 64)
        D = E // H

        def _rmsnorm(t, w):
            eps = jnp.finfo(t.dtype).eps
            return t * jax.lax.rsqrt(jnp.mean(t * t, axis=-1, keepdims=True) + eps) * w
        key = jax.random.key(seed)
        ks = jax.random.split(key, 11)
        B, T = (2, 512)
        s = 1.0 / np.sqrt(E)
        return {'x': jax.random.normal(ks[0], (B, T, E), jnp.float32), 'wq': jax.random.normal(ks[1], (E, E), jnp.float32) * s, 'bq': jnp.zeros((E,), jnp.float32), 'wk': jax.random.normal(ks[2], (E, E), jnp.float32) * s, 'bk': jnp.zeros((E,), jnp.float32), 'wv': jax.random.normal(ks[3], (E, E), jnp.float32) * s, 'bv': jnp.zeros((E,), jnp.float32), 'wo': jax.random.normal(ks[4], (E, E), jnp.float32) * s, 'bo': jnp.zeros((E,), jnp.float32), 'qn_w': jnp.ones((D,), jnp.float32), 'kn_w': jnp.ones((D,), jnp.float32)}
    _L0_attn_in = _L0_attn_setup()

    def _L0_ffn_setup():
        import jax, jax.numpy as jnp
        import numpy as np
        B, T, D, FF, E, TOP_K = (8, 512, 256, 1024, 8, 2)
        key = jax.random.key(seed)
        kx, kr, k1, k2 = jax.random.split(key, 4)
        x = jax.random.normal(kx, (B, T, D), dtype=jnp.float32)
        Wr = jax.random.normal(kr, (E, D), dtype=jnp.float32) * 0.02
        W1 = jax.random.normal(k1, (E, D, FF), dtype=jnp.float32) * 0.02
        W2 = jax.random.normal(k2, (E, FF, D), dtype=jnp.float32) * 0.02
        return {'x': x, 'Wr': Wr, 'W1': W1, 'W2': W2}
    _L0_ffn_in = _L0_ffn_setup()
    _d = {'L0_attn_x': _L0_attn_in['x'], 'L0_attn_wq': _L0_attn_in['wq'], 'L0_attn_bq': _L0_attn_in['bq'], 'L0_attn_wk': _L0_attn_in['wk'], 'L0_attn_bk': _L0_attn_in['bk'], 'L0_attn_wv': _L0_attn_in['wv'], 'L0_attn_bv': _L0_attn_in['bv'], 'L0_attn_wo': _L0_attn_in['wo'], 'L0_attn_bo': _L0_attn_in['bo'], 'L0_attn_qn_w': _L0_attn_in['qn_w'], 'L0_attn_kn_w': _L0_attn_in['kn_w'], 'L0_ffn_Wr': _L0_ffn_in['Wr'], 'L0_ffn_W1': _L0_ffn_in['W1'], 'L0_ffn_W2': _L0_ffn_in['W2']}
    _x0 = _d['L0_attn_x']
    _d['L0_attn_x'] = jax.random.normal(jax.random.fold_in(jax.random.key(seed), 1), (8, 1024, 256), dtype=_x0.dtype)
    del _x0
    return _d

def reference(L0_attn_x, L0_attn_wq, L0_attn_bq, L0_attn_wk, L0_attn_bk, L0_attn_wv, L0_attn_bv, L0_attn_wo, L0_attn_bo, L0_attn_qn_w, L0_attn_kn_w, L0_ffn_Wr, L0_ffn_W1, L0_ffn_W2):

    def _L0_attn_ref(x, wq, bq, wk, bk, wv, bv, wo, bo, qn_w, kn_w):
        import jax, jax.numpy as jnp
        import numpy as np
        E, H, W = (256, 16, 64)
        D = E // H

        def _rmsnorm(t, w):
            eps = jnp.finfo(t.dtype).eps
            return t * jax.lax.rsqrt(jnp.mean(t * t, axis=-1, keepdims=True) + eps) * w
        B, T, _ = x.shape
        q = (x @ wq + bq).reshape(B, T, H, D).transpose(0, 2, 1, 3)
        k = (x @ wk + bk).reshape(B, T, H, D).transpose(0, 2, 1, 3)
        v = (x @ wv + bv).reshape(B, T, H, D).transpose(0, 2, 1, 3)
        q = _rmsnorm(q, qn_w)
        k = _rmsnorm(k, kn_w)
        scores = jnp.einsum('bhqd,bhkd->bhqk', q, k) / jnp.sqrt(jnp.float32(D))
        row = jnp.arange(T)[:, None]
        col = jnp.arange(T)[None, :]
        invalid = (col > row) | (row - col >= W)
        neg_inf = jnp.float32(-jnp.inf)
        scores = jnp.where(invalid, neg_inf, scores)
        masked_attn = jnp.where(invalid, 0.0, jax.nn.softmax(scores, axis=-1))
        gene_means = jnp.mean(jax.nn.sigmoid(masked_attn), axis=-1)
        denom = gene_means + 0.5
        sum_inv = jnp.sum(1.0 / denom, axis=2, keepdims=True)
        fitness = 1.0 / (denom * sum_inv)
        scores = scores + jnp.log(fitness)[..., None]
        attn = jax.nn.softmax(scores, axis=-1)
        out = jnp.einsum('bhqk,bhkd->bhqd', attn, v)
        out = out.transpose(0, 2, 1, 3).reshape(B, T, E)
        return out @ wo + bo

    def _L0_ffn_ref(x, Wr, W1, W2):
        import jax, jax.numpy as jnp
        import numpy as np
        B, T, D, FF, E, TOP_K = (8, 512, 256, 1024, 8, 2)
        Bs, Ts, Ds = x.shape
        Ne = Wr.shape[0]
        xf = x.reshape(-1, Ds)
        N = xf.shape[0]
        logits = xf @ Wr.T
        topk_vals, topk_idx = jax.lax.top_k(logits, TOP_K)
        w = jax.nn.softmax(topk_vals.astype(jnp.float32), axis=-1).astype(x.dtype)
        idx_flat = topk_idx.reshape(-1)
        w_flat = w.reshape(-1)
        sort_idx = jnp.argsort(idx_flat)
        rev = sort_idx // TOP_K
        sw = w_flat[sort_idx]
        perm = xf[rev]
        S = perm.shape[0]
        chunks = perm.reshape(Ne, S // Ne, Ds)
        h = jax.nn.gelu(jnp.einsum('ecd,edf->ecf', chunks, W1), approximate=False)
        eo = jnp.einsum('ecf,efd->ecd', h, W2).reshape(S, Ds)
        out = jnp.zeros((N, Ds), dtype=x.dtype).at[rev].add(eo * sw[:, None])
        return out.reshape(Bs, Ts, Ds)
    x = L0_attn_x
    xn = _layernorm(x, axis=-1)
    x = x + _L0_attn_ref(xn, L0_attn_wq, L0_attn_bq, L0_attn_wk, L0_attn_bk, L0_attn_wv, L0_attn_bv, L0_attn_wo, L0_attn_bo, L0_attn_qn_w, L0_attn_kn_w) + _L0_ffn_ref(xn, L0_ffn_Wr, L0_ffn_W1, L0_ffn_W2)
    return x

_drawn_inputs = setup_inputs


def setup_inputs(seed=0):
    import zlib

    import numpy as np

    out = dict(_drawn_inputs(seed))
    spreads = {'L0_attn_bq': (0.0, 0.479),
     'L0_attn_bk': (0.0, 0.8),
     'L0_attn_bv': (0.0, 0.1),
     'L0_attn_bo': (0.0, 0.1),
     'L0_attn_qn_w': (1.0, 0.6),
     'L0_attn_kn_w': (1.0, 0.2)}
    factors = {}
    for name, (base, spread) in spreads.items():
        noise = np.random.default_rng([zlib.crc32(name.encode()), seed]).standard_normal(out[name].shape)
        drawn = base * np.exp(spread * noise) if base else spread * noise
        out[name] = jnp.asarray(drawn.astype(out[name].dtype))
    for name, factor in factors.items():
        out[name] = (out[name] * factor).astype(out[name].dtype)
    return out
```

```python
import concourse.bass as bass
from concourse import mybir
from contextlib import ExitStack


P = 128


def attention_and_experts(nc, x, wq, bq, wk, bk, wv, bv, wo, bo, qn_w, kn_w, Wr, W1, W2, out):
    F32, F32R, BF16, I32 = mybir.dt.float32, mybir.dt.float32r, mybir.dt.bfloat16, mybir.dt.int32
    ALU = mybir.AluOpType
    ACT = mybir.ActivationFunctionType
    AX = mybir.AxisListType

    B, T, D = x.shape
    NE, _, FF = W1.shape
    TOPK = 2
    H, WIN = 16, 64
    DH = D // H
    N = B * T
    NT = N // P
    TB = T // P
    DC = D // P
    FCH = FF // P
    ROWS = N * TOPK
    UNIT = ROWS // NT
    US = UNIT // P
    UE = (ROWS // NE) // UNIT
    assert TB == UE and B == NE and WIN * 2 == P
    HP = 4
    NU = HP * 2 * DC
    G4 = 4
    NG = NT // G4
    LN_EPS, RMS_EPS = 1e-5, 1.1920928955078125e-07
    NEG = -1.0e30

    xt = x.rearrange("b t d -> (b t) d").rearrange("(n p) d -> p n d", p=P)
    ot = out.rearrange("b t d -> (b t) d").rearrange("(n p) d -> p n d", p=P)
    routed = nc.dram_tensor("routed_rows", [ROWS + UNIT, D], F32).ap()
    expert_out = nc.dram_tensor("expert_rows", [ROWS, D], F32).ap()
    routed_t = routed.rearrange("(n p) d -> p n d", p=P)
    expert_t = expert_out.rearrange("(n p) d -> p n d", p=P)
    W1v = W1.rearrange("e (c p) f -> p e c f", p=P)
    W2v = W2.rearrange("e (f p) d -> p e f d", p=P)

    ctx = ExitStack()
    with ctx:
        def sb(name, shape, dt=F32):
            return ctx.enter_context(nc.sbuf_tensor(name, shape, dt))

        def sem(name):
            return ctx.enter_context(nc.semaphore(name))

        xn_all = sb("xn_all", [P, NT + 1, D])
        scratch = sb("scratch", [P, 2, NU * P])
        e_sb = scratch[:, 0, :].rearrange("p (u k) -> p u k", k=P)
        pT_sb = scratch[:, 1, :].rearrange("p (u k) -> p u k", k=P)
        raw = sb("raw", [P, 2, 1024])
        w1h, w1l = sb("w1h", [P, DC, FF], F32R), sb("w1l", [P, DC, FF], F32R)
        w2h, w2l = sb("w2h", [P, FCH, D], F32R), sb("w2l", [P, FCH, D], F32R)
        wqkvh, wqkvl = sb("wqkvh", [P, DC, 3 * D], F32R), sb("wqkvl", [P, DC, 3 * D], F32R)
        woh, wol = sb("woh", [P, DC, D], F32R), sb("wol", [P, DC, D], F32R)
        masks = sb("masks", [P, TB, 2, P], BF16)
        ident = sb("ident", [P, P])
        identb = sb("identb", [P, P], BF16)
        upper = sb("upper", [P, P], BF16)
        onesb = sb("onesb", [P, P], BF16)
        wr_sb = sb("wr_sb", [NE, D])
        wrT = sb("wrT", [P, DC, NE])
        qkv_bias = sb("qkv_bias", [P, 3 * D])
        bo_b = sb("bo_b", [P, D])
        nw = sb("nw", [P, 2])
        qscale = sb("qscale", [P, 2])
        minus_half = sb("minus_half", [P, 1])
        xs = sb("xs", [P, D])
        xTh, xTl = sb("xTh", [P, DC, P], F32R), sb("xTl", [P, DC, P], F32R)
        qkb = sb("qkb", [P, 2 * D])
        sq = sb("sq", [P, 2 * D])
        ss = sb("ss", [P, 2 * H])
        rms = sb("rms", [P, 2 * H])
        qh, ql = sb("qh", [P, DC * 2, 2, WIN], F32R), sb("ql", [P, DC * 2, 2, WIN], F32R)
        kh, kl = sb("kh", [P, DC, WIN + P], F32R), sb("kl", [P, DC, WIN + P], F32R)
        v0, v1 = sb("v0", [P, D]), sb("v1", [P, D])
        nmax = sb("nmax", [P, NU])
        lsum = sb("lsum", [P, NU])
        rl = sb("rl", [P, NU])
        at = sb("at", [P, D])
        aTh, aTl = sb("aTh", [P, DC, P], F32R), sb("aTl", [P, DC, P], F32R)
        xres = sb("xres", [P, D])
        xg = sb("xg", [P, US, D])
        gTh, gTl = sb("gTh", [P, DC, UNIT], F32R), sb("gTl", [P, DC, UNIT], F32R)
        hf = sb("hf", [P, 2, 2 * UNIT])
        hh, hl = sb("hh", [P, FCH, UNIT], F32R), sb("hl", [P, FCH, UNIT], F32R)
        ysb = sb("ysb", [P, US, D])
        logits = sb("logits", [P, NT, NE])
        stats = sb("stats", [P, G4, 6])
        mv = sb("mv", [P, G4, 2])
        rstd = sb("rstd", [P, G4])
        wtop = sb("wtop", [P, TOPK, NT + 2 * G4])
        pidx = sb("pidx", [P, TOPK, NT + 2 * G4], I32)
        ist = sb("ist", [P, 2, TOPK, G4], I32)
        wst = sb("wst", [P, 2, TOPK, G4])

        flat = scratch[:, :, :].rearrange("p a b -> p (a b)")
        xin = flat[:, 0:2 * G4 * D].rearrange("p (s n d) -> p s n d", s=2, d=D)
        xs4 = flat[:, 2048:2048 + G4 * D].rearrange("p (n d) -> p n d", d=D)
        xT4 = flat[:, 3072:3072 + G4 * D].rearrange("p (n c t) -> p n c t", c=DC, t=P)

        def arr(k):
            return flat[:, k * 512:(k + 1) * 512]

        xst = flat[:, 0:2 * G4 * D].rearrange("p (s n d) -> p s n d", s=2, d=D)
        gath = flat[:, 0:2 * G4 * TOPK * D].rearrange("p (s n k d) -> p s n k d", s=2, k=TOPK, d=D)
        ost = raw[:, :, :].rearrange("p s (n d) -> p s n d", d=D)

        S = ctx.enter_context(nc.psum_tensor("scores_ps", [P, HP, 512], F32))
        M = ctx.enter_context(nc.psum_tensor("attn_ps", [P, 512], F32))
        FM = ctx.enter_context(nc.psum_tensor("ffn_ps", [P, 512], F32))
        HB = ctx.enter_context(nc.psum_tensor("hidden_ps", [P, 2, 512], F32))

        names = """pool_held dve_held const_loaded weights_loaded const_made attn_hi attn_split raw_loaded0 raw_loaded1
            w_hi w_split pool_step dve_step xin_loaded0 xin_loaded1 stats_ready rstd_ready
            xs4_ready xn_kept x4_ps x4T_ready logit_ps logit_ready wr_ps sel_ready prefix_ps
            gap_ready gap_exp routed_ready staged scattered0 scattered1 pad_ready pad_written
            xs_ready xT_ps xT_ready qk_ps qk_biased sq_ready ss_ready qkn_ready v_ps v_ready
            qkT_ps khalo_ready qkT_hi qkT_ready s_ps max_ready exp_done pT_ps pT_ready pv_ps
            at_ready aT_ps aTh_ready aT_ready o_ps acc_done xres_loaded xres_ready xg_loaded
            gT_ps gTh_ready gT_ready h_ps h_evicted h_split y_ps y_evicted y_stored
            idx_staged gathered0 gathered1 combined stored0 stored1""".split()
        s = {n: sem(n) for n in names}
        raw_loaded = [s["raw_loaded0"], s["raw_loaded1"]]
        xin_loaded = [s["xin_loaded0"], s["xin_loaded1"]]
        scattered = [s["scattered0"], s["scattered1"]]
        gathered = [s["gathered0"], s["gathered1"]]
        stored = [s["stored0"], s["stored1"]]

        PIECES = 4
        N_CONST = 4 + 2 * (P // DH) + 1
        GROUP_DMAS = G4 * TOPK

        def f32(ap):
            return ap.bitcast(F32)

        def w_piece(e, k):
            if k < 2:
                return W1v[:, bass.ds(e, 1), k, :]
            return W2v[:, bass.ds(e, 1), 4 * (k - 2):4 * (k - 1), :]

        def w_part(h1, h2, k):
            if k < 2:
                return h1[:, k, :]
            return h2[:, 4 * (k - 2):4 * (k - 1), :].rearrange("p f d -> p (f d)")

        def start(engine, name, by=1):
            engine.sem_inc(s[name], by)

        block = ctx.enter_context(nc.Block())

        @block.sync
        def _(sp):
            def load(dst, src):
                sp.dma_start(dst, src).then_inc(s["const_loaded"], 16)

            start(sp, "y_stored", 16)
            for r in range(2):
                start(sp, f"stored{r}", 16)
            for k, w in enumerate((wq, wk, wv, wo)):
                sp.dma_start(raw[:, :, k * D:(k + 1) * D],
                             w.rearrange("(c p) n -> p c n", p=P)).then_inc(s["weights_loaded"], 16)
            for k, b in enumerate((bq, bk, bv)):
                load(qkv_bias[:, k * D:(k + 1) * D], b.rearrange("(o n) -> o n", o=1).to_broadcast([P, D]))
            load(bo_b[:, :], bo.rearrange("(o n) -> o n", o=1).to_broadcast([P, D]))
            for h in range(P // DH):
                load(nw[h * DH:(h + 1) * DH, 0:1], qn_w.rearrange("(n o) -> n o", o=1))
                load(nw[h * DH:(h + 1) * DH, 1:2], kn_w.rearrange("(n o) -> n o", o=1))
            load(wr_sb[:, :], Wr)

            with sp.Fori(0, NG // 2) as g2:
                for r in range(2):
                    sp.wait_ge(s["xs4_ready"], g2 * 2 + r + 1)
                    sp.dma_start(xin[:, r], xt[:, bass.ds(g2 * 2 * G4 + r * G4, G4), :]
                                 ).then_inc(xin_loaded[r], 16)

            sp.wait_ge(s["pad_ready"], 1)
            sp.dma_start(routed_t[:, NT * US:(NT + 1) * US, :], ysb[:, :, :]).then_inc(s["pad_written"], 16)

            sp.wait_ge(s["attn_split"], 2)
            for k in range(2):
                sp.dma_start(raw[:, k, :], w_piece(0, k)).then_inc(raw_loaded[k], 16)

            for r in range(2):
                sp.wait_ge(scattered[r], 16 * GROUP_DMAS * (NG // 2))
            sp.wait_ge(s["pad_written"], 16)
            sp.dma_start(xg[:, :, :], routed_t[:, 0:US, :]).then_inc(s["xg_loaded"], 16)

            with sp.Fori(0, NE) as e:
                for k in range(PIECES):
                    sp.wait_ge(s["w_split"], e * PIECES + k + 1)
                    nxt = e if k < 2 else (e + 1) % NE
                    sp.dma_start(raw[:, k % 2, :], w_piece(nxt, (k + 2) % PIECES)).then_inc(raw_loaded[k % 2], 16)
                with sp.Fori(0, UE) as j:
                    i = e * UE + j
                    sp.wait_ge(s["acc_done"], i + 1)
                    sp.dma_start(xres[:, :], xt[:, bass.ds(i, 1), :]).then_inc(s["xres_loaded"], 16)
                    sp.wait_ge(s["gT_ps"], i + 1)
                    sp.dma_start(xg[:, :, :], routed_t[:, bass.ds((i + 1) * US, US), :]
                                 ).then_inc(s["xg_loaded"], 16)
                    sp.wait_ge(s["y_evicted"], i + 1)
                    sp.dma_start(expert_t[:, bass.ds(i * US, US), :], ysb[:, :, :]).then_inc(s["y_stored"], 16)

            with sp.Fori(0, NG // 2) as g2:
                for r in range(2):
                    sp.wait_ge(s["combined"], g2 * 2 + r + 1)
                    sp.dma_start(ot[:, bass.ds(g2 * 2 * G4 + r * G4, G4), :], ost[:, r]).then_inc(stored[r], 16)
            for r in range(2):
                sp.wait_ge(stored[r], 16 * (NG // 2 + 1))
                sp.wait_ge(raw_loaded[r], 16 * (2 * NE + 1))
            sp.wait_ge(s["xg_loaded"], 16 * (NT + 1))

        @block.gpsimd
        def _(pool):
            steps = [0]

            def step(ins, base=0):
                steps[0] += 1
                ins.then_inc(s["pool_step"], 1)
                pool.wait_ge(s["pool_step"], base + steps[0])

            def wait(name, value):
                pool.wait_ge(s[name], value)
                pool.sem_inc(s["pool_held"], 1)

            start(pool, "xn_kept")
            nc.gpsimd.memset(minus_half[:, :], -0.5)
            nc.gpsimd.memset(onesb[:, :], 1.0)
            nc.gpsimd.memset(upper[:, :], 1.0)
            nc.gpsimd.memset(masks[:, :, :, :], 0.0)
            step(nc.gpsimd.memset(ident[:, :], 0.0))
            step(nc.gpsimd.affine_select(out=ident[:, :], in_=ident[:, :], pattern=[[-1, P]], base=0,
                                         compare_op=ALU.not_equal, fill=1.0, channel_multiplier=1))
            nc.gpsimd.tensor_copy(identb[:, :], ident[:, :])
            nc.gpsimd.affine_select(out=upper[:, :], in_=upper[:, :], pattern=[[1, P]], base=0,
                                    compare_op=ALU.is_gt, fill=0.0, channel_multiplier=-1)
            for h in range(2):
                m = masks[h * WIN:(h + 1) * WIN, :, :, :].rearrange("p j a c -> p (j a) c")
                step(nc.gpsimd.affine_select(out=m, in_=m, pattern=[[0, 2 * TB], [1, P]], base=0,
                                             compare_op=ALU.is_gt, fill=NEG, channel_multiplier=-1))
                step(nc.gpsimd.affine_select(out=m, in_=m, pattern=[[0, 2 * TB], [-1, P]], base=WIN,
                                             compare_op=ALU.is_ge, fill=NEG, channel_multiplier=1))
                m0 = masks[h * WIN:(h + 1) * WIN, 0, 0, :]
                step(nc.gpsimd.affine_select(out=m0, in_=m0, pattern=[[1, P]], base=-WIN,
                                             compare_op=ALU.is_ge, fill=NEG, channel_multiplier=0))
            nc.gpsimd.memset(xn_all[:, NT, :], 0.0).then_inc(s["const_made"], 1)

            base0 = steps[0]
            with pool.Fori(0, NG) as g:
                wait("stats_ready", g + 1)
                steps[0] = 0
                step(nc.gpsimd.tensor_scalar(rstd[:, :], mv[:, :, 1], LN_EPS, None, ALU.add), base0 + g)
                nc.gpsimd.tensor_tensor(rstd[:, :], rstd[:, :], minus_half[:, :].to_broadcast([P, G4]),
                                        ALU.pow).then_inc(s["rstd_ready"], 1)
                wait("xs4_ready", g + 3)
                nc.gpsimd.tensor_copy(xn_all[:, bass.ds(g * G4, G4), :], xs4).then_inc(s["xn_kept"], 1)
            base0 += NG

            with pool.Fori(0, NG // 2) as g2:
                for r in range(2):
                    wait("staged", g2 * 2 + r + 1)
                    for n in range(G4):
                        for k in range(TOPK):
                            nc.gpsimd.indirect_dma_start(
                                out=routed[0:ROWS, :], out_offset=bass.IndirectOffsetOnAxis(ap=ist[:, r, k, n:n + 1], axis=0),
                                in_=xst[:, r, n, :], in_offset=None).then_inc(scattered[r], 16)

            def stage(t):
                if not isinstance(t, int):
                    wait("xT_ps", t)
                nc.gpsimd.tensor_copy(xs[:, :], xn_all[:, bass.ds(t, 1), :]).then_inc(s["xs_ready"], 1)

            def rms_norm(t, base):
                pool.wait_ge(s["qk_biased"], t + 1)
                nc.gpsimd.tensor_tensor(sq[:, :], qkb[:, :], qkb[:, :], ALU.mult).then_inc(s["sq_ready"], 1)
                wait("ss_ready", t + 1)
                step(nc.gpsimd.tensor_scalar(rms[:, :], ss[:, :], 1.0 / DH, RMS_EPS, ALU.mult, ALU.add), base)
                step(nc.gpsimd.tensor_tensor(rms[:, :], rms[:, :], minus_half[:, :].to_broadcast([P, 2 * H]),
                                             ALU.pow), base)
                q3 = qkb[:, :].rearrange("p (h d) -> p h d", d=DH)
                nc.gpsimd.tensor_tensor(q3, q3, rms[:, :].unsqueeze(2).to_broadcast([P, 2 * H, DH]),
                                        ALU.mult).then_inc(s["qkn_ready"], 1)

            steps[0] = 0
            stage(0)
            rms_norm(0, base0)
            base0 += 2
            with pool.Fori(0, NE) as e:
                with pool.Fori(0, UE) as j:
                    i = e * UE + j
                    steps[0] = 0
                    stage(i + 1)
                    wait("xres_loaded", (i + 1) * 16)
                    nc.gpsimd.tensor_tensor(xres[:, :], xres[:, :], bo_b[:, :], ALU.add).then_inc(s["xres_ready"], 1)
                    wait("s_ps", i + 1)
                    nc.gpsimd.tensor_copy(kh[:, :, 0:WIN], f32(kh[:, :, P:P + WIN]))
                    nc.gpsimd.tensor_copy(kl[:, :, 0:WIN], f32(kl[:, :, P:P + WIN])).then_inc(s["khalo_ready"], 1)
                    rms_norm(i + 1, base0 + i * 2)

            pool.wait_ge(s["y_stored"], 16 * (NT + 1))
            with pool.Fori(0, NG // 2) as g2:
                for r in range(2):
                    wait("idx_staged", g2 * 2 + r + 1)
                    for n in range(G4):
                        for k in range(TOPK):
                            nc.gpsimd.indirect_dma_start(
                                out=gath[:, r, n, k, :], out_offset=None, in_=expert_out[:, :],
                                in_offset=bass.IndirectOffsetOnAxis(ap=ist[:, r, k, n:n + 1], axis=0)
                            ).then_inc(gathered[r], 16)

        @block.scalar
        def _(act):
            def copy(dst, src, **kw):
                return nc.scalar.activation(dst, src, ACT.Copy, **kw)

            start(act, "pT_ready")
            start(act, "h_evicted", 2)
            act.wait_ge(s["weights_loaded"], 4 * 16)
            for c in range(DC):
                copy(wqkvh[:, c, :], raw[:, c, 0:3 * D])
                copy(woh[:, c, :], raw[:, c, 3 * D:4 * D]).then_inc(s["attn_hi"], 1)
            act.wait_ge(s["wr_ps"], 1)
            copy(wrT[:, :, :], M[:, 0:DC * NE].rearrange("p (c e) -> p c e", e=NE)).then_inc(s["logit_ready"], 1)

            with act.Fori(0, NG) as g:
                act.wait_ge(s["x4_ps"], g + 2)
                copy(xT4.rearrange("p n c t -> p (n c t)"),
                     S[:, 0:2, :].rearrange("p b c -> p (b c)")).then_inc(s["x4T_ready"], 1)
                act.wait_ge(s["logit_ps"], g + 1)
                copy(logits[:, bass.ds(g * G4, G4), :],
                     M[:, 0:G4 * NE].rearrange("p (n e) -> p n e", e=NE)).then_inc(s["logit_ready"], 1)

            act.wait_ge(s["gap_ready"], 1)
            nc.scalar.activation(arr(6)[:, 0:NT], arr(5)[:, 0:NT], ACT.Exp).then_inc(s["gap_exp"], 1)

            def qk_hi(t):
                act.wait_ge(s["qkT_ps"], t + 1)
                if not isinstance(t, int):
                    act.wait_ge(s["khalo_ready"], t)
                for eo in range(2):
                    copy(qh[:, :, eo, :], M[:, 0:D].rearrange("p (u w) -> p u w", w=WIN),
                         scale=qscale[:, eo:eo + 1])
                copy(kh[:, :, WIN:WIN + P], M[:, D:2 * D].rearrange("p (g k) -> p g k", k=P)
                     ).then_inc(s["qkT_hi"], 1)

            def rows_hi(t):
                act.wait_ge(s["gT_ps"], t + 1)
                copy(gTh[:, :, :].rearrange("p c r -> p (c r)"), FM[:, :]).then_inc(s["gTh_ready"], 1)

            rows_hi(0)
            qk_hi(0)
            with act.Fori(0, NE) as e:
                act.wait_ge(s["y_ps"], e * UE + 1)
                for k in range(PIECES):
                    act.wait_ge(raw_loaded[k % 2], (e * 2 + k // 2 + 1) * 16)
                    copy(w_part(w1h, w2h, k), raw[:, k % 2, :]).then_inc(s["w_hi"], 1)
                with act.Fori(0, UE) as j:
                    i = e * UE + j
                    for q in range(4):
                        act.wait_ge(s["h_ps"], i * 4 + q + 1)
                        act.wait_ge(s["h_split"], i * 4 + q + 1)
                        nc.scalar.activation(hf[:, q % 2, :], HB[:, q % 2, :], ACT.Gelu).then_inc(s["h_evicted"], 1)
                    act.wait_ge(s["max_ready"], i + 1)
                    for u in range(NU):
                        jj, ag = u // 4, u % 4
                        last = nc.scalar.activation(e_sb[:, u, :], S[:, jj, ag * P:(ag + 1) * P], ACT.Exp,
                                                    bias=nmax[:, u:u + 1], accum_out=lsum[:, u:u + 1])
                    last.then_inc(s["exp_done"], 1)
                    act.wait_ge(s["pT_ps"], i + 1)
                    copy(scratch[:, 1, :], S[:, :, :].rearrange("p b c -> p (b c)")).then_inc(s["pT_ready"], 1)
                    act.wait_ge(s["y_ps"], i + 2)
                    act.wait_ge(s["y_stored"], (i + 1) * 16)
                    copy(ysb[:, :, :].rearrange("p n d -> p (n d)"), FM[:, :]).then_inc(s["y_evicted"], 1)
                    rows_hi(i + 1)
                    act.wait_ge(s["aT_ps"], i + 1)
                    copy(aTh[:, :, :].rearrange("p c t -> p (c t)"), M[:, 0:D]).then_inc(s["aTh_ready"], 1)
                    qk_hi(i + 1)

        @block.vector
        def _(dve):
            V = nc.vector
            steps = [0]

            def step(ins, base=0):
                steps[0] += 1
                ins.then_inc(s["dve_step"], 1)
                dve.wait_ge(s["dve_step"], base + steps[0])

            start(dve, "xs4_ready", 2)
            start(dve, "h_split", 2)
            start(dve, "acc_done")
            V.memset(v1[:, :], 0.0)
            V.memset(f32(kh[:, :, :]), 0.0)
            V.memset(f32(kl[:, :, :]), 0.0)
            V.memset(pidx[:, :, NT:], 0)
            V.memset(wtop[:, :, NT:], 0.0)
            V.memset(ysb[:, :, :], 0.0).then_inc(s["pad_ready"], 1)

            for c in range(DC):
                dve.wait_ge(s["attn_hi"], c + 1)
                V.tensor_tensor(wqkvl[:, c, :], raw[:, c, 0:3 * D], f32(wqkvh[:, c, :]), ALU.subtract)
                V.tensor_tensor(wol[:, c, :], raw[:, c, 3 * D:4 * D], f32(woh[:, c, :]),
                                ALU.subtract).then_inc(s["attn_split"], 1)

            dve.wait_ge(s["const_made"], 1)
            dve.wait_ge(s["const_loaded"], 16 * N_CONST)
            V.tensor_reduce(qscale[:, :], ident[:, :].rearrange("p (j e d) -> p e j d", j=HP, e=2), AX.XY, ALU.add)
            step(V.tensor_tensor(nw[:, 0:1], nw[:, 0:1], nw[:, 1:2], ALU.mult))
            step(V.tensor_scalar(qscale[:, :], qscale[:, :], nw[:, 0:1], DH ** -0.5, ALU.mult, ALU.mult))

            with dve.Fori(0, NG // 2) as g2:
                for r in range(2):
                    g = g2 * 2 + r
                    dve.wait_ge(xin_loaded[r], (g2 + 1) * 16)
                    for n in range(G4):
                        last = V.bn_stats(stats[:, n, :], xin[:, r, n, :])
                    last.then_inc(s["dve_step"], 1)
                    dve.wait_ge(s["dve_step"], g + (2 + 1))
                    dve.sem_inc(s["dve_held"], 1)
                    for n in range(G4):
                        last = V.bn_aggr(mv[:, n, :], stats[:, n, :])
                    last.then_inc(s["stats_ready"], 1)
                    dve.wait_ge(s["rstd_ready"], g + 1)
                    dve.wait_ge(s["xn_kept"], g + 1)
                    dve.wait_ge(s["x4_ps"], g + 1)
                    for n in range(G4):
                        last = V.tensor_scalar(xs4[:, n, :], xin[:, r, n, :], mv[:, n, 0:1], rstd[:, n:n + 1],
                                               ALU.subtract, ALU.mult)
                    last.then_inc(s["xs4_ready"], 1)
            base = 2 + NG

            dve.wait_ge(s["logit_ready"], NG + 1)
            dve.wait_ge(s["xn_kept"], NG + 1)
            L = logits[:, :, :]
            rank = arr(0).rearrange("p (n e) -> p n e", e=NE)
            tmp = arr(1).rearrange("p (n e) -> p n e", e=NE)
            top = [arr(2).rearrange("p (n e) -> p n e", e=NE), arr(3).rearrange("p (n e) -> p n e", e=NE)]
            steps[0] = 0
            step(V.memset(arr(0), 0.0), base)
            for o in range(NE):
                if o:
                    step(V.tensor_tensor(tmp[:, :, 0:o], L[:, :, o:o + 1].to_broadcast([P, NT, o]), L[:, :, 0:o],
                                         ALU.is_gt), base)
                if o < NE - 1:
                    step(V.tensor_tensor(tmp[:, :, o + 1:NE], L[:, :, o:o + 1].to_broadcast([P, NT, NE - 1 - o]),
                                         L[:, :, o + 1:NE], ALU.is_ge), base)
                step(V.memset(tmp[:, :, o:o + 1], 0.0), base)
                step(V.tensor_tensor(rank, rank, tmp, ALU.add), base)
            for k in range(TOPK):
                step(V.tensor_scalar(top[k], rank, float(k), None, ALU.is_equal), base)
            sel = arr(4)[:, 0:256].bitcast(BF16).rearrange("p (e n) -> p e n", e=NE)
            V.tensor_scalar(sel.rearrange("p e n -> p n e"), rank, float(TOPK) - 0.5, None,
                            ALU.is_lt).then_inc(s["sel_ready"], 1)
            lt = [arr(5)[:, 64 * (k + 1):64 * (k + 2)] for k in range(TOPK)]
            for k in range(TOPK):
                step(V.tensor_tensor(tmp, top[k], L, ALU.mult), base)
                step(V.tensor_reduce(lt[k], tmp, AX.X, ALU.add), base)
            V.tensor_tensor(arr(5)[:, 0:NT], lt[1], lt[0], ALU.subtract).then_inc(s["gap_ready"], 1)
            dve.wait_ge(s["gap_exp"], 1)
            eB = arr(6)[:, 0:NT]
            step(V.tensor_scalar(arr(6)[:, 64:128], eB, 1.0, None, ALU.add), base)
            step(V.reciprocal(wtop[:, 0, 0:NT], arr(6)[:, 64:128]), base)
            V.tensor_tensor(wtop[:, 1, 0:NT], wtop[:, 0, 0:NT], eB, ALU.mult)
            dve.wait_ge(s["prefix_ps"], 1)
            ones512 = arr(0)
            step(V.memset(ones512, 1.0), base)
            step(V.tensor_tensor_scan(arr(7), ones512, S[:, 1, :], 0.0, ALU.mult, ALU.add), base)
            step(V.tensor_tensor(arr(7), arr(7), S[:, 1, :], ALU.subtract), base)
            step(V.tensor_tensor(arr(7), arr(7), S[:, 0, :], ALU.add), base)
            pos = arr(7).rearrange("p (e n) -> p n e", e=NE)
            for k in range(TOPK):
                step(V.tensor_tensor(tmp, top[k], pos, ALU.mult), base)
                step(V.tensor_reduce(lt[k], tmp, AX.X, ALU.add), base)
                step(V.tensor_copy(pidx[:, k, 0:NT], lt[k]), base)
            base += steps[0]

            def stage_rows(g, r):
                V.tensor_copy(ist[:, r, :, :], pidx[:, :, bass.ds(g * G4, G4)])
                V.tensor_copy(xst[:, r], xn_all[:, bass.ds(g * G4, G4), :]).then_inc(s["staged"], 1)

            for r in range(2):
                stage_rows(r, r)
            with dve.Fori(1, NG // 2) as g2:
                for r in range(2):
                    dve.wait_ge(scattered[r], g2 * (16 * GROUP_DMAS))
                    stage_rows(g2 * 2 + r, r)

            def hi_lo_x(t):
                dve.wait_ge(s["xT_ps"], t + 1)
                ps = M[:, 0:D].rearrange("p (c k) -> p c k", k=P)
                step(V.tensor_copy(xTh[:, :, :], ps), cur[0])
                V.tensor_tensor(xTl[:, :, :], ps, f32(xTh[:, :, :]), ALU.subtract).then_inc(s["xT_ready"], 1)

            def bias_qk(t):
                dve.wait_ge(s["qk_ps"], t + 1)
                V.tensor_tensor(qkb[:, :], M[:, :], qkv_bias[:, 0:2 * D], ALU.add).then_inc(s["qk_biased"], 1)

            def square_sums(t):
                dve.wait_ge(s["sq_ready"], t + 1)
                V.tensor_reduce(ss[:, :], sq[:, :].rearrange("p (h d) -> p h d", d=DH), AX.X,
                                ALU.add).then_inc(s["ss_ready"], 1)

            def values(t):
                dve.wait_ge(s["v_ps"], t + 1)
                bv_b = qkv_bias[:, 2 * D:3 * D]
                step(V.tensor_copy(v0[0:WIN, :], v1[WIN:P, :]), cur[0])
                V.tensor_tensor(v0[WIN:P, :], M[0:WIN, 0:D], bv_b[0:WIN, :], ALU.add)
                V.tensor_tensor(v1[:, :], M[:, 0:D], bv_b, ALU.add).then_inc(s["v_ready"], 1)

            def rows_lo(t):
                dve.wait_ge(s["gTh_ready"], t + 1)
                V.tensor_tensor(gTl[:, :, :].rearrange("p c r -> p (c r)"), FM[:, :],
                                f32(gTh[:, :, :].rearrange("p c r -> p (c r)")), ALU.subtract).then_inc(s["gT_ready"], 1)

            def qk_lo(t):
                dve.wait_ge(s["qkT_hi"], t + 1)
                for eo in range(2):
                    V.scalar_tensor_tensor(ql[:, :, eo, :], M[:, 0:D].rearrange("p (u w) -> p u w", w=WIN),
                                           qscale[:, eo:eo + 1], f32(qh[:, :, eo, :]), ALU.mult, ALU.subtract)
                V.tensor_tensor(kl[:, :, WIN:WIN + P], M[:, D:2 * D].rearrange("p (g k) -> p g k", k=P),
                                f32(kh[:, :, WIN:WIN + P]), ALU.subtract).then_inc(s["qkT_ready"], 1)

            cur = [base]
            steps[0] = 0
            hi_lo_x(0)
            bias_qk(0)
            square_sums(0)
            values(0)
            rows_lo(0)
            qk_lo(0)
            base += steps[0]
            PER = 1 + 1 + 1 + 4
            with dve.Fori(0, NE) as e:
                for k in range(PIECES):
                    dve.wait_ge(s["w_hi"], e * PIECES + k + 1)
                    V.tensor_tensor(w_part(w1l, w2l, k), raw[:, k % 2, :], f32(w_part(w1h, w2h, k)),
                                    ALU.subtract).then_inc(s["w_split"], 1)
                with dve.Fori(0, UE) as j:
                    i = e * UE + j
                    cur[0] = i * PER + base
                    steps[0] = 0

                    def split(q):
                        dve.wait_ge(s["h_evicted"], i * 4 + q + 3)
                        f = hf[:, q % 2, :].rearrange("p (n r) -> p n r", n=2)
                        step(V.tensor_copy(hh[:, 2 * q:2 * q + 2, :], f), cur[0])
                        V.tensor_tensor(hl[:, 2 * q:2 * q + 2, :], f, f32(hh[:, 2 * q:2 * q + 2, :]),
                                        ALU.subtract).then_inc(s["h_split"], 1)

                    split(0)
                    split(1)
                    dve.wait_ge(s["s_ps"], i + 1)
                    V.tensor_reduce(nmax[:, :], S[:, :, :].rearrange("p j (u k) -> p (j u) k", k=P), AX.X, ALU.max,
                                    negate=True).then_inc(s["max_ready"], 1)
                    split(2)
                    split(3)
                    hi_lo_x(i + 1)
                    bias_qk(i + 1)
                    square_sums(i + 1)
                    dve.wait_ge(s["exp_done"], i + 1)
                    step(V.reciprocal(rl[:, :], lsum[:, :]), cur[0])
                    dve.wait_ge(s["pv_ps"], i + 1)
                    for a in range(2):
                        for eo in range(2):
                            q = slice(eo * WIN, (eo + 1) * WIN)
                            src = M[q, :].rearrange("p (j a g e d) -> p j a g e d", j=HP, a=2, g=DC, e=2)[:, :, a, :, eo, :]
                            inv = rl[q, :].rearrange("p (j a g) -> p j a g", j=HP, a=2)[:, :, a, :]
                            dst = at[a * WIN:(a + 1) * WIN, :].rearrange("p (g j e d) -> p j g e d", g=DC, j=HP, e=2)[:, :, :, eo, :]
                            last = V.tensor_tensor(dst, src, inv.unsqueeze(3).to_broadcast([WIN, HP, DC, DH]), ALU.mult)
                    last.then_inc(s["at_ready"], 1)
                    values(i + 1)
                    rows_lo(i + 1)
                    dve.wait_ge(s["aTh_ready"], i + 1)
                    V.tensor_tensor(aTl[:, :, :].rearrange("p c t -> p (c t)"), M[:, 0:D],
                                    f32(aTh[:, :, :].rearrange("p c t -> p (c t)")), ALU.subtract).then_inc(s["aT_ready"], 1)
                    dve.wait_ge(s["o_ps"], i + 1)
                    dve.wait_ge(s["xres_ready"], i + 1)
                    V.tensor_tensor(xn_all[:, bass.ds(i, 1), :], M[:, 0:D].unsqueeze(1), xres[:, :].unsqueeze(1),
                                    ALU.add).then_inc(s["acc_done"], 1)
                    qk_lo(i + 1)
            assert steps[0] == PER
            base += PER * NT

            def stage_idx(g, r):
                V.tensor_copy(ist[:, r, :, :], pidx[:, :, bass.ds(g * G4, G4)])
                V.tensor_copy(wst[:, r, :, :], wtop[:, :, bass.ds(g * G4, G4)]).then_inc(s["idx_staged"], 1)

            for r in range(2):
                stage_idx(r, r)
            with dve.Fori(0, NG // 2) as g2:
                for r in range(2):
                    g = g2 * 2 + r
                    dve.wait_ge(gathered[r], (g2 + 1) * (16 * GROUP_DMAS))
                    dve.wait_ge(stored[r], (g2 + 1) * 16)
                    for n in range(G4):
                        last = V.scalar_tensor_tensor(ost[:, r, n:n + 1, :], gath[:, r, n, 0:1, :], wst[:, r, 0, n:n + 1],
                                                      xn_all[:, bass.ds(g * G4 + n, 1), :], ALU.mult, ALU.add)
                    last.then_inc(s["dve_step"], 1)
                    dve.wait_ge(s["dve_step"], g + (base + 1))
                    for n in range(G4):
                        last = V.scalar_tensor_tensor(ost[:, r, n, :], gath[:, r, n, 1, :], wst[:, r, 1, n:n + 1],
                                                      ost[:, r, n, :], ALU.mult, ALU.add)
                    last.then_inc(s["combined"], 1)
                    dve.wait_ge(s["combined"], g + 1)
                    stage_idx(g + 2, r)

        @block.tensor
        def _(pe):
            MM = nc.tensor.matmul

            def split_product(dst, ah, al, bh, bl, n, start=True, stop=True):
                for c in range(n):
                    for k, (a, b) in enumerate(((ah, bh), (al, bh), (ah, bl))):
                        last = MM(dst, a(c), b(c), start=(start and c == 0 and k == 0), stop=(stop and c == n - 1 and k == 2))
                return last

            start(pe, "y_ps")
            start(pe, "x4_ps")
            pe.wait_ge(s["const_made"], 1)
            pe.wait_ge(s["const_loaded"], 16 * N_CONST)
            for c in range(DC):
                last = nc.tensor.transpose(M[:, c * NE:(c + 1) * NE], wr_sb[:, c * P:(c + 1) * P], ident[0:NE, 0:NE])
            last.then_inc(s["wr_ps"], 1)

            with pe.Fori(0, NG) as g:
                pe.wait_ge(s["xs4_ready"], g + 3)
                for n in range(G4):
                    for c in range(DC):
                        k = n * DC + c
                        last = nc.tensor.transpose(S[:, k // 4, (k % 4) * P:(k % 4 + 1) * P], xs4[:, n, c * P:(c + 1) * P], ident[:, :])
                last.then_inc(s["x4_ps"], 1)
                pe.wait_ge(s["x4T_ready"], g + 1)
                pe.wait_ge(s["logit_ready"], g + 1)
                for n in range(G4):
                    for c in range(DC):
                        last = MM(M[:, n * NE:(n + 1) * NE], xT4[:, n, c, :], wrT[:, c, :], start=(c == 0), stop=(c == DC - 1))
                last.then_inc(s["logit_ps"], 1)

            pe.wait_ge(s["sel_ready"], 1)
            sel = arr(4)[:, 0:256].bitcast(BF16)
            MM(S[:, 0, :], upper[:, :], sel, start=True, stop=True)
            MM(S[:, 1, :], onesb[:, :], sel, start=True, stop=True).then_inc(s["prefix_ps"], 1)

            def transpose_x(t):
                pe.wait_ge(s["xs_ready"], t + 1)
                for c in range(DC):
                    last = nc.tensor.transpose(M[:, c * P:(c + 1) * P], xs[:, c * P:(c + 1) * P], ident[:, :])
                last.then_inc(s["xT_ps"], 1)

            def project_qk(t):
                pe.wait_ge(s["xT_ready"], t + 1)
                split_product(M[:, :], lambda c: xTh[:, c, :], lambda c: xTl[:, c, :],
                              lambda c: wqkvh[:, c, 0:2 * D], lambda c: wqkvl[:, c, 0:2 * D], DC).then_inc(s["qk_ps"], 1)

            def project_v(t):
                split_product(M[:, 0:D], lambda c: xTh[:, c, :], lambda c: xTl[:, c, :],
                              lambda c: wqkvh[:, c, 2 * D:3 * D], lambda c: wqkvl[:, c, 2 * D:3 * D], DC).then_inc(s["v_ps"], 1)

            def transpose_rows(t):
                pe.wait_ge(s["xg_loaded"], (t + 1) * 16)
                for c in range(DC):
                    for n in range(US):
                        k = c * US + n
                        last = nc.tensor.transpose(FM[:, k * P:(k + 1) * P], xg[:, n, c * P:(c + 1) * P], ident[:, :])
                last.then_inc(s["gT_ps"], 1)

            def transpose_qk(t):
                pe.wait_ge(s["qkn_ready"], t + 1)
                for k in range(4):
                    last = nc.tensor.transpose(M[:, k * P:(k + 1) * P], qkb[:, k * P:(k + 1) * P], ident[:, :])
                last.then_inc(s["qkT_ps"], 1)

            pe.wait_ge(s["logit_ready"], NG + 1)
            pe.wait_ge(s["attn_split"], 2)
            transpose_x(0)
            project_qk(0)
            pe.wait_ge(s["qk_biased"], 1)
            project_v(0)
            transpose_rows(0)
            pe.wait_ge(s["v_ready"], 1)
            transpose_qk(0)

            with pe.Fori(0, NE) as e:
                with pe.Fori(0, UE) as j:
                    i = e * UE + j

                    def hidden(q):
                        pe.wait_ge(s["h_evicted"], i * 4 + q + 1)
                        for f in (2 * q, 2 * q + 1):
                            last = split_product(HB[:, q % 2, (f % 2) * UNIT:(f % 2 + 1) * UNIT],
                                                 lambda c: w1h[:, c, f * P:(f + 1) * P], lambda c: w1l[:, c, f * P:(f + 1) * P],
                                                 lambda c: gTh[:, c, :], lambda c: gTl[:, c, :], DC)
                        last.then_inc(s["h_ps"], 1)

                    def expert(n, f0, f1):
                        return split_product(FM[:, n * D:(n + 1) * D],
                                             lambda c: hh[:, f0 + c, n * P:(n + 1) * P], lambda c: hl[:, f0 + c, n * P:(n + 1) * P],
                                             lambda c: w2h[:, f0 + c, :], lambda c: w2l[:, f0 + c, :], f1 - f0,
                                             start=(f0 == 0), stop=(f1 == FCH))

                    pe.wait_ge(s["w_split"], e * PIECES + 2)
                    pe.wait_ge(s["gT_ready"], i + 1)
                    hidden(0)
                    hidden(1)
                    pe.wait_ge(s["qkT_ready"], i + 1)
                    pe.wait_ge(s["pT_ready"], i + 1)
                    for jj in range(HP):
                        MM(S[:, jj, :], identb[:, :], masks[:, bass.ds(j, 1), :, :].rearrange("p o a c -> p (o a) c")
                           .unsqueeze(2).to_broadcast([P, 2, DC, P]), start=True, stop=False)
                    for a in range(2):
                        for g in range(DC):
                            for k, (qq, kk) in enumerate(((qh, kh), (ql, kh), (qh, kl))):
                                for jj in range(HP):
                                    r = slice(32 * jj, 32 * jj + 32)
                                    ag = a * DC + g
                                    last = MM(S[:, jj, ag * P:(ag + 1) * P],
                                              qq[r, g * 2 + a, :, :].rearrange("p e w -> p (e w)"),
                                              kk[r, g, a * WIN:a * WIN + P], start=False, stop=(ag == 3 and k == 2))
                    last.then_inc(s["s_ps"], 1)
                    hidden(2)
                    hidden(3)
                    transpose_x(i + 1)
                    project_qk(i + 1)
                    pe.wait_ge(s["h_split"], i * 4 + 6)
                    pe.wait_ge(s["w_split"], e * PIECES + 4)
                    expert(0, 0, FCH)
                    pe.wait_ge(s["exp_done"], i + 1)
                    for u in range(NU):
                        last = nc.tensor.transpose(S[:, u // 4, (u % 4) * P:(u % 4 + 1) * P], e_sb[:, u, :], ident[:, :])
                    last.then_inc(s["pT_ps"], 1)
                    expert(1, 0, FCH // 2)
                    pe.wait_ge(s["pT_ready"], i + 2)
                    pe.wait_ge(s["qk_biased"], i + 2)
                    for u in range(NU):
                        jj, a, g = u // 4, (u // 2) % 2, u % 2
                        last = MM(M[:, u * 32:(u + 1) * 32], pT_sb[:, u, :], (v0, v1)[a][:, g * P + jj * 32:g * P + jj * 32 + 32],
                                  start=True, stop=True)
                    last.then_inc(s["pv_ps"], 1)
                    expert(1, FCH // 2, FCH).then_inc(s["y_ps"], 1)
                    pe.wait_ge(s["at_ready"], i + 1)
                    project_v(i + 1)
                    pe.wait_ge(s["y_evicted"], i + 1)
                    transpose_rows(i + 1)
                    pe.wait_ge(s["v_ready"], i + 2)
                    for c in range(DC):
                        last = nc.tensor.transpose(M[:, c * P:(c + 1) * P], at[:, c * P:(c + 1) * P], ident[:, :])
                    last.then_inc(s["aT_ps"], 1)
                    pe.wait_ge(s["aT_ready"], i + 1)
                    split_product(M[:, 0:D], lambda c: aTh[:, c, :], lambda c: aTl[:, c, :],
                                  lambda c: woh[:, c, :], lambda c: wol[:, c, :], DC).then_inc(s["o_ps"], 1)
                    pe.wait_ge(s["acc_done"], i + 2)
                    transpose_qk(i + 1)


_INS = ["L0_attn_x", "L0_attn_wq", "L0_attn_bq", "L0_attn_wk", "L0_attn_bk", "L0_attn_wv", "L0_attn_bv", "L0_attn_wo",
        "L0_attn_bo", "L0_attn_qn_w", "L0_attn_kn_w", "L0_ffn_Wr", "L0_ffn_W1", "L0_ffn_W2"]


def kernel(**inputs):
    import numpy as _np
    import concourse.bacc as _bacc
    from concourse import mybir as _mybir
    from concourse.bass_utils import run_bass_kernel_spmd as _run

    nc = _bacc.Bacc("TRN2", target_bir_lowering=False, num_devices=1)
    arrays, args = {}, []
    for name in _INS:
        a = _np.ascontiguousarray(inputs[name])
        arrays[f"in_{name}_dram"] = a
        args.append(nc.dram_tensor(f"in_{name}_dram", a.shape, _mybir.dt.from_np(a.dtype), kind="ExternalInput").ap())
    shape = tuple(inputs["L0_attn_x"].shape)
    args.append(nc.dram_tensor("out_0_dram", shape, _mybir.dt.float32, kind="ExternalOutput").ap())
    attention_and_experts(nc, *args)
    r = _run(nc, [arrays], core_ids=[0])
    return r.results[0]["out_0_dram"]
```

```python
import concourse.bass as bass
from concourse import mybir
from contextlib import ExitStack


P = 128


def attention_and_experts(nc, x, wq, bq, wk, bk, wv, bv, wo, bo, qn_w, kn_w, Wr, W1, W2, out):
    F32, F32R, BF16, I32 = mybir.dt.float32, mybir.dt.float32r, mybir.dt.bfloat16, mybir.dt.int32
    ALU = mybir.AluOpType
    ACT = mybir.ActivationFunctionType
    AX = mybir.AxisListType

    B, T, D = x.shape
    NE, _, FF = W1.shape
    TOPK = 2
    H, WIN = 16, 64
    DH = D // H
    N = B * T
    NT = N // P
    TB = T // P
    DC = D // P
    FCH = FF // P
    ROWS = N * TOPK
    UNIT = ROWS // NT
    US = UNIT // P
    UE = (ROWS // NE) // UNIT
    assert TB == UE and B == NE and WIN * 2 == P
    HP = 4
    NP = H // 2
    NU = HP * 2 * DC
    G4 = 4
    NG = NT // G4
    LN_EPS, RMS_EPS = 1e-5, 1.1920928955078125e-07
    NEG = -1.0e30

    xt = x.rearrange("b t d -> (b t) d").rearrange("(n p) d -> p n d", p=P)
    ot = out.rearrange("b t d -> (b t) d").rearrange("(n p) d -> p n d", p=P)
    routed = nc.dram_tensor("routed_rows", [ROWS + UNIT, D], F32).ap()
    expert_out = nc.dram_tensor("expert_rows", [ROWS, D], F32).ap()
    routed_t = routed.rearrange("(n p) d -> p n d", p=P)
    expert_t = expert_out.rearrange("(n p) d -> p n d", p=P)
    W1v = W1.rearrange("e (c p) f -> p e c f", p=P)
    W2v = W2.rearrange("e (f p) d -> p e f d", p=P)

    ctx = ExitStack()
    with ctx:
        def sb(name, shape, dt=F32):
            return ctx.enter_context(nc.sbuf_tensor(name, shape, dt))

        def sem(name):
            return ctx.enter_context(nc.semaphore(name))

        xn_all = sb("xn_all", [P, NT + 2, D])
        scratch = sb("scratch", [P, 2, NU * P])
        e_sb = scratch[:, 0, :].rearrange("p (u k) -> p u k", k=P)
        pT_sb = scratch[:, 1, :].rearrange("p (u k) -> p u k", k=P)
        raw = sb("raw", [P, 2, 1024])
        w1h, w1l = sb("w1h", [P, DC, FF], F32R), sb("w1l", [P, DC, FF], F32R)
        w2h, w2l = sb("w2h", [P, FCH, D], F32R), sb("w2l", [P, FCH, D], F32R)
        wqkvh, wqkvl = sb("wqkvh", [P, DC, 3 * D], F32R), sb("wqkvl", [P, DC, 3 * D], F32R)
        woh, wol = sb("woh", [P, DC, D], F32R), sb("wol", [P, DC, D], F32R)
        masks = sb("masks", [P, TB, 2, P], BF16)
        ident = sb("ident", [P, P])
        identb = sb("identb", [P, P], BF16)
        upper = sb("upper", [P, P], BF16)
        onesb = sb("onesb", [P, P], BF16)
        wr_sb = sb("wr_sb", [NE, D])
        wrT = sb("wrT", [P, DC, NE])
        qkv_bias = sb("qkv_bias", [P, 3 * D])
        bo_b = sb("bo_b", [P, D])
        nw = sb("nw", [P, 2, DH])
        qw = sb("qw", [P, DH])
        minus_half = sb("minus_half", [P, 1])
        xs = sb("xs", [P, D])
        xTh, xTl = sb("xTh", [P, DC, P], F32R), sb("xTl", [P, DC, P], F32R)
        qkb = sb("qkb", [P, 2 * D])
        sq = sb("sq", [P, 2 * D])
        ss = sb("ss", [P, 2 * H])
        rms = sb("rms", [P, 2 * H])
        qT = sb("qT", [P, NP, 2, 2, WIN], F32R)
        kT = sb("kT", [P, NP, WIN + P], F32R)
        v0, v1 = sb("v0", [P, D]), sb("v1", [P, D])
        nmax = sb("nmax", [P, NU])
        lsum = sb("lsum", [P, NU])
        rl = sb("rl", [P, NU])
        at = sb("at", [P, D])
        aTh, aTl = sb("aTh", [P, DC, P], F32R), sb("aTl", [P, DC, P], F32R)
        xres = sb("xres", [P, D])
        xg = sb("xg", [P, US, D])
        gTh, gTl = sb("gTh", [P, DC, UNIT], F32R), sb("gTl", [P, DC, UNIT], F32R)
        hf = sb("hf", [P, 2, 2 * UNIT])
        hh, hl = sb("hh", [P, FCH, UNIT], F32R), sb("hl", [P, FCH, UNIT], F32R)
        ysb = sb("ysb", [P, US, D])
        logits = sb("logits", [P, NT, NE])
        stats = sb("stats", [P, G4, 6])
        mv = sb("mv", [P, G4, 2])
        rstd = sb("rstd", [P, G4])
        wtop = sb("wtop", [P, TOPK, NT + 2 * G4])
        pidx = sb("pidx", [P, TOPK, NT + 2 * G4], I32)
        ist = sb("ist", [P, 2, TOPK, G4], I32)
        wst = sb("wst", [P, 2, TOPK, G4])

        flat = scratch[:, :, :].rearrange("p a b -> p (a b)")
        xin = flat[:, 0:2 * G4 * D].rearrange("p (s n d) -> p s n d", s=2, d=D)
        xs4 = flat[:, 2048:2048 + G4 * D].rearrange("p (n d) -> p n d", d=D)
        xT4 = flat[:, 3072:3072 + G4 * D].rearrange("p (n c t) -> p n c t", c=DC, t=P)

        def arr(k):
            return flat[:, k * 512:(k + 1) * 512]

        qk4 = scratch[:, 0, :].rearrange("p (s h x y d) -> p s h x y d", s=2, h=H, x=2, y=2)

        xst = flat[:, 2048:2048 + 2 * G4 * D].rearrange("p (s n d) -> p s n d", s=2, d=D)
        gath = flat[:, 0:2 * G4 * TOPK * D].rearrange("p (s n k d) -> p s n k d", s=2, k=TOPK, d=D)
        ost = raw[:, :, :].rearrange("p s (n d) -> p s n d", d=D)

        S = ctx.enter_context(nc.psum_tensor("scores_ps", [P, HP, 512], F32))
        M = ctx.enter_context(nc.psum_tensor("attn_ps", [P, 512], F32))
        FM = ctx.enter_context(nc.psum_tensor("ffn_ps", [P, 512], F32))
        HB = ctx.enter_context(nc.psum_tensor("hidden_ps", [P, 2, 512], F32))

        names = """pool_held dve_held const_loaded weights_loaded const_made attn_hi attn_split raw_loaded0 raw_loaded1
            w_hi w_split pool_step dve_step xin_loaded0 xin_loaded1 stats_ready rstd_ready
            xs4_ready xn_kept x4_ps x4T_ready logit_ps logit_ready wr_ps sel_ready prefix_ps
            gap_ready gap_exp staged scattered0 scattered1 pad_ready pad_written
            xs_ready xT_ps xT_ready qk_ps qk_biased sq_ready ss_ready qw_ready qkn_ready v_ps v_ready
            qk4_hi qk4_ready qkT_ps khalo_ready qkT_even qkT_odd s_ps max_ready exp_done pT_ps pT_low
            pT_high pv_ps at_ready aT_ps aTh_ready aT_ready o_ps acc_done xres_loaded xres_ready
            xg_loaded gT_ps gTh_ready gT_ready h_ps h_evicted h_split y_ps y_evicted y_stored
            idx_staged gathered0 gathered1 combined stored0 stored1""".split()
        s = {n: sem(n) for n in names}
        raw_loaded = [s["raw_loaded0"], s["raw_loaded1"]]
        xin_loaded = [s["xin_loaded0"], s["xin_loaded1"]]
        scattered = [s["scattered0"], s["scattered1"]]
        gathered = [s["gathered0"], s["gathered1"]]
        stored = [s["stored0"], s["stored1"]]

        PIECES = 4
        N_CONST = 4 + 2 + 1
        GROUP_DMAS = G4 * TOPK

        def f32(ap):
            return ap.bitcast(F32)

        def w_piece(e, k):
            if k < 2:
                return W1v[:, bass.ds(e, 1), k, :]
            return W2v[:, bass.ds(e, 1), 4 * (k - 2):4 * (k - 1), :]

        def w_part(h1, h2, k):
            if k < 2:
                return h1[:, k, :]
            return h2[:, 4 * (k - 2):4 * (k - 1), :].rearrange("p f d -> p (f d)")

        def start(engine, name, by=1):
            engine.sem_inc(s[name], by)

        block = ctx.enter_context(nc.Block())

        @block.sync
        def _(sp):
            def load(dst, src):
                sp.dma_start(dst, src).then_inc(s["const_loaded"], 16)

            start(sp, "y_stored", 16)
            for r in range(2):
                start(sp, f"stored{r}", 16)
            for k, w in enumerate((wq, wk, wv, wo)):
                sp.dma_start(raw[:, :, k * D:(k + 1) * D],
                             w.rearrange("(c p) n -> p c n", p=P)).then_inc(s["weights_loaded"], 16)
            for k, b in enumerate((bq, bk, bv)):
                load(qkv_bias[:, k * D:(k + 1) * D], b.rearrange("(o n) -> o n", o=1).to_broadcast([P, D]))
            load(bo_b[:, :], bo.rearrange("(o n) -> o n", o=1).to_broadcast([P, D]))
            for k, w in enumerate((qn_w, kn_w)):
                load(nw[:, k, :], w.rearrange("(o n) -> o n", o=1).to_broadcast([P, DH]))
            load(wr_sb[:, :], Wr)

            with sp.Fori(0, NG // 2) as g2:
                for r in range(2):
                    sp.wait_ge(s["xs4_ready"], g2 * 2 + r + 1)
                    sp.dma_start(xin[:, r], xt[:, bass.ds(g2 * 2 * G4 + r * G4, G4), :]
                                 ).then_inc(xin_loaded[r], 16)

            sp.wait_ge(s["pad_ready"], 1)
            sp.dma_start(routed_t[:, NT * US:(NT + 1) * US, :], ysb[:, :, :]).then_inc(s["pad_written"], 16)

            def load_piece(e, k):
                sp.dma_start(raw[:, k % 2, :], w_piece(e, k)).then_inc(raw_loaded[k % 2], 16)

            sp.wait_ge(s["attn_split"], 2)
            load_piece(0, 0)
            load_piece(0, 1)
            for k in range(PIECES):
                sp.wait_ge(s["w_split"], k + 1)
                load_piece(k // 2, (k + 2) % PIECES)

            for r in range(2):
                sp.wait_ge(scattered[r], 16 * GROUP_DMAS * (NG // 2))
            sp.wait_ge(s["pad_written"], 16)
            sp.dma_start(xg[:, :, :], routed_t[:, 0:US, :]).then_inc(s["xg_loaded"], 16)

            with sp.Fori(0, NE) as e:
                def turn(i, last):
                    sp.wait_ge(s["gT_ps"], i + 1)
                    sp.dma_start(xg[:, :, :], routed_t[:, bass.ds((i + 1) * US, US), :]
                                 ).then_inc(s["xg_loaded"], 16)
                    sp.wait_ge(s["acc_done"], i + 1)
                    sp.dma_start(xres[:, :], xt[:, bass.ds(i, 1), :]).then_inc(s["xres_loaded"], 16)
                    if last:
                        for k in range(2):
                            sp.wait_ge(s["w_split"], (e + 1) * PIECES + k + 1)
                            load_piece((e + 1) % NE, k + 2)
                    sp.wait_ge(s["y_evicted"], i + 2)
                    sp.dma_start(expert_t[:, bass.ds(i * US, US), :], ysb[:, :, :]).then_inc(s["y_stored"], 16)
                    if last:
                        for k in range(2):
                            sp.wait_ge(s["w_split"], (e + 1) * PIECES + k + 3)
                            load_piece((e + 2) % NE, k)

                with sp.Fori(0, UE - 1) as j:
                    turn(e * UE + j, False)
                turn(e * UE + (UE - 1), True)

            with sp.Fori(0, NG // 2) as g2:
                for r in range(2):
                    sp.wait_ge(s["combined"], g2 * 2 + r + 1)
                    sp.dma_start(ot[:, bass.ds(g2 * 2 * G4 + r * G4, G4), :], ost[:, r]).then_inc(stored[r], 16)
            for r in range(2):
                sp.wait_ge(stored[r], 16 * (NG // 2 + 1))
                sp.wait_ge(raw_loaded[r], 16 * (2 * NE + 3))
            sp.wait_ge(s["xg_loaded"], 16 * (NT + 1))

        @block.gpsimd
        def _(pool):
            steps = [0]

            def step(ins, base=0):
                steps[0] += 1
                ins.then_inc(s["pool_step"], 1)
                pool.wait_ge(s["pool_step"], base + steps[0])

            def wait(name, value):
                pool.wait_ge(s[name], value)
                pool.sem_inc(s["pool_held"], 1)

            start(pool, "xn_kept")
            nc.gpsimd.memset(minus_half[:, :], -0.5)
            nc.gpsimd.memset(onesb[:, :], 1.0)
            nc.gpsimd.memset(upper[:, :], 1.0)
            nc.gpsimd.memset(masks[:, :, :, :], 0.0)
            step(nc.gpsimd.memset(ident[:, :], 0.0))
            step(nc.gpsimd.affine_select(out=ident[:, :], in_=ident[:, :], pattern=[[-1, P]], base=0,
                                         compare_op=ALU.not_equal, fill=1.0, channel_multiplier=1))
            nc.gpsimd.tensor_copy(identb[:, :], ident[:, :])
            nc.gpsimd.affine_select(out=upper[:, :], in_=upper[:, :], pattern=[[1, P]], base=0,
                                    compare_op=ALU.is_gt, fill=0.0, channel_multiplier=-1)
            for h in range(2):
                m = masks[h * WIN:(h + 1) * WIN, :, :, :].rearrange("p j a c -> p (j a) c")
                step(nc.gpsimd.affine_select(out=m, in_=m, pattern=[[0, 2 * TB], [1, P]], base=0,
                                             compare_op=ALU.is_gt, fill=NEG, channel_multiplier=-1))
                step(nc.gpsimd.affine_select(out=m, in_=m, pattern=[[0, 2 * TB], [-1, P]], base=WIN,
                                             compare_op=ALU.is_ge, fill=NEG, channel_multiplier=1))
                m0 = masks[h * WIN:(h + 1) * WIN, 0, 0, :]
                step(nc.gpsimd.affine_select(out=m0, in_=m0, pattern=[[1, P]], base=-WIN,
                                             compare_op=ALU.is_ge, fill=NEG, channel_multiplier=0))
            nc.gpsimd.memset(xn_all[:, NT:, :], 0.0).then_inc(s["const_made"], 1)

            base0 = steps[0]
            with pool.Fori(0, NG) as g:
                wait("stats_ready", g + 1)
                steps[0] = 0
                step(nc.gpsimd.tensor_scalar(rstd[:, :], mv[:, :, 1], LN_EPS, None, ALU.add), base0 + g)
                nc.gpsimd.tensor_tensor(rstd[:, :], rstd[:, :], minus_half[:, :].to_broadcast([P, G4]),
                                        ALU.pow).then_inc(s["rstd_ready"], 1)
                wait("xs4_ready", g + 3)
                nc.gpsimd.tensor_copy(xn_all[:, bass.ds(g * G4, G4), :], xs4).then_inc(s["xn_kept"], 1)
            base0 += NG

            def stage(t):
                if not (isinstance(t, int) and t == 0):
                    wait("xT_ps", t)
                nc.gpsimd.tensor_copy(xs[:, :], xn_all[:, bass.ds(t, 1), :]).then_inc(s["xs_ready"], 1)

            def rms_norm(t, base):
                pool.wait_ge(s["qk_biased"], t + 1)
                nc.gpsimd.tensor_tensor(sq[:, :], qkb[:, :], qkb[:, :], ALU.mult).then_inc(s["sq_ready"], 1)
                wait("ss_ready", t + 1)
                step(nc.gpsimd.tensor_scalar(rms[:, :], ss[:, :], 1.0 / DH, RMS_EPS, ALU.mult, ALU.add), base)
                step(nc.gpsimd.tensor_tensor(rms[:, :], rms[:, :], minus_half[:, :].to_broadcast([P, 2 * H]),
                                             ALU.pow), base)
                pool.wait_ge(s["qw_ready"], t + 1)
                q3 = qkb[:, :].rearrange("p (h d) -> p h d", d=DH)
                nc.gpsimd.tensor_tensor(q3, q3, rms[:, :].unsqueeze(2).to_broadcast([P, 2 * H, DH]),
                                        ALU.mult).then_inc(s["qkn_ready"], 1)

            steps[0] = 0
            stage(0)
            rms_norm(0, base0)
            stage(1)
            base0 += 2

            with pool.Fori(0, NG // 2) as g2:
                for r in range(2):
                    wait("staged", g2 * 2 + r + 1)
                    for n in range(G4):
                        for k in range(TOPK):
                            nc.gpsimd.indirect_dma_start(
                                out=routed[0:ROWS, :], out_offset=bass.IndirectOffsetOnAxis(ap=ist[:, r, k, n:n + 1], axis=0),
                                in_=xst[:, r, n, :], in_offset=None).then_inc(scattered[r], 16)

            with pool.Fori(0, NT) as i:
                steps[0] = 0
                wait("s_ps", i + 1)
                nc.gpsimd.tensor_copy(kT[:, :, 0:WIN], f32(kT[:, :, P:P + WIN])).then_inc(s["khalo_ready"], 1)
                wait("xres_loaded", (i + 1) * 16)
                nc.gpsimd.tensor_tensor(xres[:, :], xres[:, :], bo_b[:, :], ALU.add).then_inc(s["xres_ready"], 1)
                rms_norm(i + 1, base0 + i * 2)
                stage(i + 2)

            pool.wait_ge(s["y_stored"], 16 * (NT + 1))
            with pool.Fori(0, NG // 2) as g2:
                for r in range(2):
                    wait("idx_staged", g2 * 2 + r + 1)
                    for n in range(G4):
                        for k in range(TOPK):
                            nc.gpsimd.indirect_dma_start(
                                out=gath[:, r, n, k, :], out_offset=None, in_=expert_out[:, :],
                                in_offset=bass.IndirectOffsetOnAxis(ap=ist[:, r, k, n:n + 1], axis=0)
                            ).then_inc(gathered[r], 16)

        @block.scalar
        def _(act):
            def copy(dst, src, **kw):
                return nc.scalar.activation(dst, src, ACT.Copy, **kw)

            start(act, "pT_high")
            start(act, "h_evicted", 2)
            act.wait_ge(s["weights_loaded"], 4 * 16)
            for c in range(DC):
                copy(wqkvh[:, c, :], raw[:, c, 0:3 * D])
                copy(woh[:, c, :], raw[:, c, 3 * D:4 * D]).then_inc(s["attn_hi"], 1)
            act.wait_ge(s["wr_ps"], 1)
            copy(wrT[:, :, :], M[:, 0:DC * NE].rearrange("p (c e) -> p c e", e=NE)).then_inc(s["logit_ready"], 1)

            with act.Fori(0, NG) as g:
                act.wait_ge(s["x4_ps"], g + 2)
                copy(xT4.rearrange("p n c t -> p (n c t)"),
                     S[:, 0:2, :].rearrange("p b c -> p (b c)")).then_inc(s["x4T_ready"], 1)
                act.wait_ge(s["logit_ps"], g + 1)
                copy(logits[:, bass.ds(g * G4, G4), :],
                     M[:, 0:G4 * NE].rearrange("p (n e) -> p n e", e=NE)).then_inc(s["logit_ready"], 1)

            act.wait_ge(s["gap_ready"], 1)
            nc.scalar.activation(arr(6)[:, 0:NT], arr(5)[:, 0:NT], ACT.Exp).then_inc(s["gap_exp"], 1)

            def parts_hi(t):
                act.wait_ge(s["qkn_ready"], t + 1)
                for k in range(2):
                    src = qkb[:, k * D:(k + 1) * D].rearrange("p (h d) -> p h d", d=DH).unsqueeze(2).to_broadcast([P, H, 2, DH])
                    dst = qk4[:, 0, :, 0, :, :] if k == 0 else qk4[:, 1, :, :, 0, :]
                    copy(dst.bitcast(F32R), src).then_inc(s["qk4_hi"], 1)

            def keep_qk(t):
                for k in range(2):
                    act.wait_ge(s["qkT_ps"], t * 2 + 1 + k)
                    if k == 0:
                        for eo in range(2):
                            h = slice(eo * WIN, (eo + 1) * WIN)
                            copy(qT[h, 0:HP, :, eo, :], S[h, 0, :].rearrange("p (n a w) -> p n a w", a=2, w=WIN))
                    else:
                        if not isinstance(t, int):
                            act.wait_ge(s["khalo_ready"], t)
                        copy(kT[:, 0:HP, WIN:WIN + P], S[:, 2, :].rearrange("p (n k) -> p n k", k=P)
                             ).then_inc(s["qkT_even"], 1)

            def rows_hi(t):
                act.wait_ge(s["gT_ps"], t + 1)
                copy(gTh[:, :, :].rearrange("p c r -> p (c r)"), HB[:, 0, :]).then_inc(s["gTh_ready"], 1)

            def weights_hi(e, k):
                act.wait_ge(raw_loaded[k % 2], (e * 2 + k // 2 + 1) * 16)
                copy(w_part(w1h, w2h, k), raw[:, k % 2, :]).then_inc(s["w_hi"], 1)

            def gelu(u, q):
                act.wait_ge(s["h_ps"], u * 4 + q + 1)
                act.wait_ge(s["h_split"], u * 4 + q + 1)
                nc.scalar.activation(hf[:, q % 2, :], HB[:, q % 2, :], ACT.Gelu).then_inc(s["h_evicted"], 1)

            for k in range(PIECES):
                weights_hi(0, k)
            act.wait_ge(s["staged"], 1)
            parts_hi(0)
            keep_qk(0)
            rows_hi(0)
            for q in range(4):
                gelu(0, q)
            with act.Fori(0, NE) as e:
                def turn(i, last):
                    if last:
                        weights_hi(e + 1, 0)
                        weights_hi(e + 1, 1)
                    rows_hi(i + 1)
                    act.wait_ge(s["max_ready"], i + 1)
                    for u in range(NU):
                        jj, ag = u // 4, u % 4
                        ex = nc.scalar.activation(e_sb[:, u, :], S[:, jj, ag * P:(ag + 1) * P], ACT.Exp,
                                                  bias=nmax[:, u:u + 1], accum_out=lsum[:, u:u + 1])
                        if u % (NU // 2) == NU // 2 - 1:
                            ex.then_inc(s["exp_done"], 1)
                    act.wait_ge(s["pT_ps"], i * 2 + 2)
                    copy(scratch[:, 1, NU * P // 2:], S[:, 2:4, :].rearrange("p b c -> p (b c)")).then_inc(s["pT_high"], 1)
                    gelu(i + 1, 0)
                    parts_hi(i + 1)
                    keep_qk(i + 1)
                    gelu(i + 1, 1)
                    if last:
                        act.wait_ge(s["y_ps"], i + 1)
                        weights_hi(e + 1, 2)
                        weights_hi(e + 1, 3)
                    act.wait_ge(s["aT_ps"], i + 1)
                    copy(aTh[:, :, :].rearrange("p c t -> p (c t)"), M[:, D:2 * D]).then_inc(s["aTh_ready"], 1)
                    gelu(i + 1, 2)
                    gelu(i + 1, 3)

                with act.Fori(0, UE - 1) as j:
                    turn(e * UE + j, False)
                turn(e * UE + (UE - 1), True)

        @block.vector
        def _(dve):
            V = nc.vector
            steps = [0]

            def step(ins, base=0):
                steps[0] += 1
                ins.then_inc(s["dve_step"], 1)
                dve.wait_ge(s["dve_step"], base + steps[0])

            start(dve, "xs4_ready", 2)
            start(dve, "h_split", 2)
            start(dve, "acc_done")
            start(dve, "pT_low")
            start(dve, "y_evicted")
            V.memset(v1[:, :], 0.0)
            V.memset(f32(kT[:, :, :]), 0.0)
            V.memset(f32(qT[:, :, :, :, :]), 0.0)
            V.memset(pidx[:, :, NT:], 0)
            V.memset(wtop[:, :, NT:], 0.0)
            V.memset(ysb[:, :, :], 0.0).then_inc(s["pad_ready"], 1)

            for c in range(DC):
                dve.wait_ge(s["attn_hi"], c + 1)
                V.tensor_tensor(wqkvl[:, c, :], raw[:, c, 0:3 * D], f32(wqkvh[:, c, :]), ALU.subtract)
                V.tensor_tensor(wol[:, c, :], raw[:, c, 3 * D:4 * D], f32(woh[:, c, :]),
                                ALU.subtract).then_inc(s["attn_split"], 1)

            dve.wait_ge(s["const_made"], 1)
            dve.wait_ge(s["const_loaded"], 16 * N_CONST)
            step(V.tensor_tensor(qw[:, :], nw[:, 0, :], nw[:, 1, :], ALU.mult))
            step(V.tensor_scalar(qw[:, :], qw[:, :], DH ** -0.5, None, ALU.mult))

            with dve.Fori(0, NG // 2) as g2:
                for r in range(2):
                    g = g2 * 2 + r
                    dve.wait_ge(xin_loaded[r], (g2 + 1) * 16)
                    for n in range(G4):
                        last = V.bn_stats(stats[:, n, :], xin[:, r, n, :])
                    last.then_inc(s["dve_step"], 1)
                    dve.wait_ge(s["dve_step"], g + (2 + 1))
                    dve.sem_inc(s["dve_held"], 1)
                    for n in range(G4):
                        last = V.bn_aggr(mv[:, n, :], stats[:, n, :])
                    last.then_inc(s["stats_ready"], 1)
                    dve.wait_ge(s["rstd_ready"], g + 1)
                    dve.wait_ge(s["xn_kept"], g + 1)
                    dve.wait_ge(s["x4_ps"], g + 1)
                    for n in range(G4):
                        last = V.tensor_scalar(xs4[:, n, :], xin[:, r, n, :], mv[:, n, 0:1], rstd[:, n:n + 1],
                                               ALU.subtract, ALU.mult)
                    last.then_inc(s["xs4_ready"], 1)
            base = 2 + NG

            def hi_lo_x(t):
                dve.wait_ge(s["xT_ps"], t + 1)
                ps = M[:, 0:D].rearrange("p (c k) -> p c k", k=P)
                step(V.tensor_copy(xTh[:, :, :], ps), cur[0])
                V.tensor_tensor(xTl[:, :, :], ps, f32(xTh[:, :, :]), ALU.subtract).then_inc(s["xT_ready"], 1)

            def bias_qk(t):
                dve.wait_ge(s["qk_ps"], t + 1)
                V.tensor_tensor(qkb[:, :], M[:, :], qkv_bias[:, 0:2 * D], ALU.add).then_inc(s["qk_biased"], 1)

            def square_sums(t):
                dve.wait_ge(s["sq_ready"], t + 1)
                V.tensor_reduce(ss[:, :], sq[:, :].rearrange("p (h d) -> p h d", d=DH), AX.X,
                                ALU.add).then_inc(s["ss_ready"], 1)
                q3 = qkb[:, 0:D].rearrange("p (h d) -> p h d", d=DH)
                V.tensor_tensor(q3, q3, qw[:, :].unsqueeze(1).to_broadcast([P, H, DH]), ALU.mult).then_inc(s["qw_ready"], 1)

            def parts_lo(t):
                for k in range(2):
                    dve.wait_ge(s["qk4_hi"], t * 2 + k + 1)
                    src = qkb[:, k * D:(k + 1) * D].rearrange("p (h d) -> p h d", d=DH).unsqueeze(2).to_broadcast([P, H, 2, DH])
                    hi = qk4[:, 0, :, 0, :, :] if k == 0 else qk4[:, 1, :, :, 0, :]
                    lo = qk4[:, 0, :, 1, :, :] if k == 0 else qk4[:, 1, :, :, 1, :]
                    V.tensor_tensor(lo.bitcast(F32R), src, hi, ALU.subtract).then_inc(s["qk4_ready"], 1)

            def keep_qk(t):
                for k in range(2):
                    dve.wait_ge(s["qkT_ps"], t * 2 + 1 + k)
                    if k == 0:
                        for eo in range(2):
                            h = slice(eo * WIN, (eo + 1) * WIN)
                            V.tensor_copy(qT[h, HP:NP, :, eo, :], S[h, 1, :].rearrange("p (n a w) -> p n a w", a=2, w=WIN))
                    else:
                        if not isinstance(t, int):
                            dve.wait_ge(s["khalo_ready"], t)
                        V.tensor_copy(kT[:, HP:NP, WIN:WIN + P], S[:, 3, :].rearrange("p (n k) -> p n k", k=P)
                                      ).then_inc(s["qkT_odd"], 1)

            def values(t):
                dve.wait_ge(s["v_ps"], t + 1)
                bv_b = qkv_bias[:, 2 * D:3 * D]
                step(V.tensor_copy(v0[0:WIN, :], v1[WIN:P, :]), cur[0])
                V.tensor_tensor(v0[WIN:P, :], M[0:WIN, 0:D], bv_b[0:WIN, :], ALU.add)
                V.tensor_tensor(v1[:, :], M[:, 0:D], bv_b, ALU.add).then_inc(s["v_ready"], 1)

            def rows_lo(t):
                dve.wait_ge(s["gTh_ready"], t + 1)
                V.tensor_tensor(gTl[:, :, :].rearrange("p c r -> p (c r)"), HB[:, 0, :],
                                f32(gTh[:, :, :].rearrange("p c r -> p (c r)")), ALU.subtract).then_inc(s["gT_ready"], 1)

            def weights_lo(e, k):
                dve.wait_ge(s["w_hi"], e * PIECES + k + 1)
                V.tensor_tensor(w_part(w1l, w2l, k), raw[:, k % 2, :], f32(w_part(w1h, w2h, k)),
                                ALU.subtract).then_inc(s["w_split"], 1)

            def split(u, q):
                dve.wait_ge(s["h_evicted"], u * 4 + q + 3)
                f = hf[:, q % 2, :].rearrange("p (n r) -> p n r", n=2)
                step(V.tensor_copy(hh[:, 2 * q:2 * q + 2, :], f), cur[0])
                V.tensor_tensor(hl[:, 2 * q:2 * q + 2, :], f, f32(hh[:, 2 * q:2 * q + 2, :]),
                                ALU.subtract).then_inc(s["h_split"], 1)

            steps[0] = 0
            cur = [base]
            hi_lo_x(0)

            dve.wait_ge(s["logit_ready"], NG + 1)
            dve.wait_ge(s["xn_kept"], NG + 1)
            L = logits[:, :, :]
            rank = arr(0).rearrange("p (n e) -> p n e", e=NE)
            tmp = arr(1).rearrange("p (n e) -> p n e", e=NE)
            top = [arr(2).rearrange("p (n e) -> p n e", e=NE), arr(3).rearrange("p (n e) -> p n e", e=NE)]
            step(V.memset(arr(0), 0.0), base)
            for o in range(NE):
                if o:
                    step(V.tensor_tensor(tmp[:, :, 0:o], L[:, :, o:o + 1].to_broadcast([P, NT, o]), L[:, :, 0:o],
                                         ALU.is_gt), base)
                if o < NE - 1:
                    step(V.tensor_tensor(tmp[:, :, o + 1:NE], L[:, :, o:o + 1].to_broadcast([P, NT, NE - 1 - o]),
                                         L[:, :, o + 1:NE], ALU.is_ge), base)
                step(V.memset(tmp[:, :, o:o + 1], 0.0), base)
                step(V.tensor_tensor(rank, rank, tmp, ALU.add), base)
            for k in range(TOPK):
                step(V.tensor_scalar(top[k], rank, float(k), None, ALU.is_equal), base)
            sel = arr(4)[:, 0:256].bitcast(BF16).rearrange("p (e n) -> p e n", e=NE)
            V.tensor_scalar(sel.rearrange("p e n -> p n e"), rank, float(TOPK) - 0.5, None,
                            ALU.is_lt).then_inc(s["sel_ready"], 1)
            bias_qk(0)
            lt = [arr(5)[:, 64 * (k + 1):64 * (k + 2)] for k in range(TOPK)]
            for k in range(TOPK):
                step(V.tensor_tensor(tmp, top[k], L, ALU.mult), base)
                step(V.tensor_reduce(lt[k], tmp, AX.X, ALU.add), base)
            V.tensor_tensor(arr(5)[:, 0:NT], lt[1], lt[0], ALU.subtract).then_inc(s["gap_ready"], 1)
            dve.wait_ge(s["gap_exp"], 1)
            eB = arr(6)[:, 0:NT]
            step(V.tensor_scalar(arr(6)[:, 64:128], eB, 1.0, None, ALU.add), base)
            step(V.reciprocal(wtop[:, 0, 0:NT], arr(6)[:, 64:128]), base)
            V.tensor_tensor(wtop[:, 1, 0:NT], wtop[:, 0, 0:NT], eB, ALU.mult)
            square_sums(0)
            dve.wait_ge(s["prefix_ps"], 1)
            ones512 = arr(0)
            step(V.memset(ones512, 1.0), base)
            step(V.tensor_tensor_scan(arr(7), ones512, S[:, 1, :], 0.0, ALU.mult, ALU.add), base)
            step(V.tensor_tensor(arr(7), arr(7), S[:, 1, :], ALU.subtract), base)
            step(V.tensor_tensor(arr(7), arr(7), S[:, 0, :], ALU.add), base)
            pos = arr(7).rearrange("p (e n) -> p n e", e=NE)
            for k in range(TOPK):
                step(V.tensor_tensor(tmp, top[k], pos, ALU.mult), base)
                step(V.tensor_reduce(lt[k], tmp, AX.X, ALU.add), base)
                step(V.tensor_copy(pidx[:, k, 0:NT], lt[k]), base)

            def stage_rows(g, r):
                V.tensor_copy(ist[:, r, :, :], pidx[:, :, bass.ds(g * G4, G4)])
                V.tensor_copy(xst[:, r], xn_all[:, bass.ds(g * G4, G4), :]).then_inc(s["staged"], 1)

            for r in range(2):
                stage_rows(r, r)

            for k in range(PIECES):
                weights_lo(0, k)
            values(0)
            parts_lo(0)
            keep_qk(0)
            with dve.Fori(1, NG // 2) as g2:
                for r in range(2):
                    dve.wait_ge(scattered[r], g2 * (16 * GROUP_DMAS))
                    stage_rows(g2 * 2 + r, r)
            rows_lo(0)
            for q in range(4):
                split(0, q)
            hi_lo_x(1)
            base += steps[0]
            PER = 1 + 1 + 1 + 4
            with dve.Fori(0, NE) as e:
                def turn(i, last):
                    cur[0] = i * PER + base
                    steps[0] = 0
                    dve.wait_ge(s["s_ps"], i + 1)
                    V.tensor_reduce(nmax[:, :], S[:, :, :].rearrange("p j (u k) -> p (j u) k", k=P), AX.X, ALU.max,
                                    negate=True).then_inc(s["max_ready"], 1)
                    bias_qk(i + 1)
                    if last:
                        weights_lo(e + 1, 0)
                        weights_lo(e + 1, 1)
                    rows_lo(i + 1)
                    square_sums(i + 1)
                    dve.wait_ge(s["y_ps"], i + 1)
                    dve.wait_ge(s["y_stored"], (i + 1) * 16)
                    V.tensor_copy(ysb[:, :, :].rearrange("p n d -> p (n d)"), FM[:, :]).then_inc(s["y_evicted"], 1)
                    dve.wait_ge(s["pT_ps"], i * 2 + 1)
                    V.tensor_copy(scratch[:, 1, 0:NU * P // 2], S[:, 0:2, :].rearrange("p b c -> p (b c)")
                                  ).then_inc(s["pT_low"], 1)
                    dve.wait_ge(s["exp_done"], i * 2 + 2)
                    step(V.reciprocal(rl[:, :], lsum[:, :]), cur[0])
                    split(i + 1, 0)
                    parts_lo(i + 1)
                    dve.wait_ge(s["pv_ps"], i + 1)
                    for a in range(2):
                        for eo in range(2):
                            q = slice(eo * WIN, (eo + 1) * WIN)
                            src = M[q, :].rearrange("p (j a g e d) -> p j a g e d", j=HP, a=2, g=DC, e=2)[:, :, a, :, eo, :]
                            inv = rl[q, :].rearrange("p (j a g) -> p j a g", j=HP, a=2)[:, :, a, :]
                            dst = at[a * WIN:(a + 1) * WIN, :].rearrange("p (g j e d) -> p j g e d", g=DC, j=HP, e=2)[:, :, :, eo, :]
                            out_h = V.tensor_tensor(dst, src, inv.unsqueeze(3).to_broadcast([WIN, HP, DC, DH]), ALU.mult)
                    out_h.then_inc(s["at_ready"], 1)
                    keep_qk(i + 1)
                    values(i + 1)
                    split(i + 1, 1)
                    if last:
                        weights_lo(e + 1, 2)
                        weights_lo(e + 1, 3)
                    dve.wait_ge(s["aTh_ready"], i + 1)
                    V.tensor_tensor(aTl[:, :, :].rearrange("p c t -> p (c t)"), M[:, D:2 * D],
                                    f32(aTh[:, :, :].rearrange("p c t -> p (c t)")), ALU.subtract).then_inc(s["aT_ready"], 1)
                    split(i + 1, 2)
                    dve.wait_ge(s["o_ps"], i + 1)
                    dve.wait_ge(s["xres_ready"], i + 1)
                    V.tensor_tensor(xn_all[:, bass.ds(i, 1), :], M[:, 0:D].unsqueeze(1), xres[:, :].unsqueeze(1),
                                    ALU.add).then_inc(s["acc_done"], 1)
                    hi_lo_x(i + 2)
                    split(i + 1, 3)
                    assert steps[0] == PER

                with dve.Fori(0, UE - 1) as j:
                    turn(e * UE + j, False)
                turn(e * UE + (UE - 1), True)
            base += PER * NT

            def stage_idx(g, r):
                V.tensor_copy(ist[:, r, :, :], pidx[:, :, bass.ds(g * G4, G4)])
                V.tensor_copy(wst[:, r, :, :], wtop[:, :, bass.ds(g * G4, G4)]).then_inc(s["idx_staged"], 1)

            for r in range(2):
                stage_idx(r, r)
                dve.wait_ge(raw_loaded[r], 16 * (2 * NE + 3))
            with dve.Fori(0, NG // 2) as g2:
                for r in range(2):
                    g = g2 * 2 + r
                    dve.wait_ge(gathered[r], (g2 + 1) * (16 * GROUP_DMAS))
                    dve.wait_ge(stored[r], (g2 + 1) * 16)
                    for n in range(G4):
                        last = V.scalar_tensor_tensor(ost[:, r, n:n + 1, :], gath[:, r, n, 0:1, :], wst[:, r, 0, n:n + 1],
                                                      xn_all[:, bass.ds(g * G4 + n, 1), :], ALU.mult, ALU.add)
                    last.then_inc(s["dve_step"], 1)
                    dve.wait_ge(s["dve_step"], g + (base + 1))
                    for n in range(G4):
                        last = V.scalar_tensor_tensor(ost[:, r, n, :], gath[:, r, n, 1, :], wst[:, r, 1, n:n + 1],
                                                      ost[:, r, n, :], ALU.mult, ALU.add)
                    last.then_inc(s["combined"], 1)
                    dve.wait_ge(s["combined"], g + 1)
                    stage_idx(g + 2, r)

        @block.tensor
        def _(pe):
            MM = nc.tensor.matmul

            def split_product(dst, ah, al, bh, bl, n, start=True, stop=True):
                for c in range(n):
                    for k, (a, b) in enumerate(((ah, bh), (al, bh), (ah, bl))):
                        last = MM(dst, a(c), b(c), start=(start and c == 0 and k == 0), stop=(stop and c == n - 1 and k == 2))
                return last

            start(pe, "x4_ps")
            pe.wait_ge(s["const_made"], 1)
            pe.wait_ge(s["const_loaded"], 16 * N_CONST)
            for c in range(DC):
                last = nc.tensor.transpose(M[:, c * NE:(c + 1) * NE], wr_sb[:, c * P:(c + 1) * P], ident[0:NE, 0:NE])
            last.then_inc(s["wr_ps"], 1)

            with pe.Fori(0, NG) as g:
                pe.wait_ge(s["xs4_ready"], g + 3)
                for n in range(G4):
                    for c in range(DC):
                        k = n * DC + c
                        last = nc.tensor.transpose(S[:, k // 4, (k % 4) * P:(k % 4 + 1) * P], xs4[:, n, c * P:(c + 1) * P], ident[:, :])
                last.then_inc(s["x4_ps"], 1)
                pe.wait_ge(s["x4T_ready"], g + 1)
                pe.wait_ge(s["logit_ready"], g + 1)
                for n in range(G4):
                    for c in range(DC):
                        last = MM(M[:, n * NE:(n + 1) * NE], xT4[:, n, c, :], wrT[:, c, :], start=(c == 0), stop=(c == DC - 1))
                last.then_inc(s["logit_ps"], 1)

            def transpose_x(t):
                pe.wait_ge(s["xs_ready"], t + 1)
                for c in range(DC):
                    last = nc.tensor.transpose(M[:, c * P:(c + 1) * P], xs[:, c * P:(c + 1) * P], ident[:, :])
                last.then_inc(s["xT_ps"], 1)

            pe.wait_ge(s["logit_ready"], NG + 1)
            transpose_x(0)

            pe.wait_ge(s["sel_ready"], 1)
            sel = arr(4)[:, 0:256].bitcast(BF16)
            MM(S[:, 0, :], upper[:, :], sel, start=True, stop=True)
            MM(S[:, 1, :], onesb[:, :], sel, start=True, stop=True).then_inc(s["prefix_ps"], 1)

            def project_qk(t):
                pe.wait_ge(s["xT_ready"], t + 1)
                split_product(M[:, :], lambda c: xTh[:, c, :], lambda c: xTl[:, c, :],
                              lambda c: wqkvh[:, c, 0:2 * D], lambda c: wqkvl[:, c, 0:2 * D], DC).then_inc(s["qk_ps"], 1)

            def project_v(t):
                split_product(M[:, 0:D], lambda c: xTh[:, c, :], lambda c: xTl[:, c, :],
                              lambda c: wqkvh[:, c, 2 * D:3 * D], lambda c: wqkvl[:, c, 2 * D:3 * D], DC).then_inc(s["v_ps"], 1)

            def transpose_rows(t):
                pe.wait_ge(s["xg_loaded"], (t + 1) * 16)
                if not isinstance(t, int):
                    pe.wait_ge(s["h_evicted"], t * 4 + 1)
                for c in range(DC):
                    for n in range(US):
                        k = c * US + n
                        last = nc.tensor.transpose(HB[:, 0, k * P:(k + 1) * P], xg[:, n, c * P:(c + 1) * P], ident[:, :])
                last.then_inc(s["gT_ps"], 1)

            def transpose_qk(t):
                for k in range(2):
                    pe.wait_ge(s["qk4_ready"], t * 2 + k + 1)
                    for n in range(NP):
                        last = nc.tensor.transpose(S[:, 2 * k + n // HP, (n % HP) * P:(n % HP + 1) * P],
                                                   scratch[:, 0, (k * NP + n) * P:(k * NP + n + 1) * P], ident[:, :])
                    last.then_inc(s["qkT_ps"], 1)

            def hidden(u, q):
                pe.wait_ge(s["h_evicted"], u * 4 + q + 1)
                for f in (2 * q, 2 * q + 1):
                    last = split_product(HB[:, q % 2, (f % 2) * UNIT:(f % 2 + 1) * UNIT],
                                         lambda c: w1h[:, c, f * P:(f + 1) * P], lambda c: w1l[:, c, f * P:(f + 1) * P],
                                         lambda c: gTh[:, c, :], lambda c: gTl[:, c, :], DC)
                last.then_inc(s["h_ps"], 1)

            def expert(n):
                return split_product(FM[:, n * D:(n + 1) * D],
                                     lambda c: hh[:, c, n * P:(n + 1) * P], lambda c: hl[:, c, n * P:(n + 1) * P],
                                     lambda c: w2h[:, c, :], lambda c: w2l[:, c, :], FCH)

            pe.wait_ge(s["attn_split"], 2)
            project_qk(0)
            pe.wait_ge(s["qk_biased"], 1)
            project_v(0)
            transpose_qk(0)
            transpose_rows(0)
            pe.wait_ge(s["w_split"], 2)
            pe.wait_ge(s["gT_ready"], 1)
            for q in range(4):
                hidden(0, q)
            pe.wait_ge(s["v_ready"], 1)
            transpose_x(1)

            with pe.Fori(0, NE) as e:
                def turn(j, last_turn):
                    i = e * UE + j
                    pe.wait_ge(s["qkT_even"], i + 1)
                    pe.wait_ge(s["qkT_odd"], i + 1)
                    for jj in range(HP):
                        MM(S[:, jj, :], identb[:, :], masks[:, bass.ds(j, 1), :, :].rearrange("p o a c -> p (o a) c")
                           .unsqueeze(2).to_broadcast([P, 2, DC, P]), start=True, stop=False)
                    for a in range(2):
                        for g in range(DC):
                            for jj in range(HP):
                                ag = a * DC + g
                                last = MM(S[:, jj, ag * P:(ag + 1) * P],
                                          qT[:, g * HP + jj, a, :, :].rearrange("p e w -> p (e w)"),
                                          kT[:, g * HP + jj, a * WIN:a * WIN + P], start=False, stop=(ag == 3))
                    last.then_inc(s["s_ps"], 1)
                    project_qk(i + 1)
                    transpose_rows(i + 1)
                    pe.wait_ge(s["h_split"], i * 4 + 6)
                    pe.wait_ge(s["w_split"], e * PIECES + 4)
                    pe.wait_ge(s["y_evicted"], i + 1)
                    expert(0)
                    expert(1).then_inc(s["y_ps"], 1)
                    for half in range(2):
                        pe.wait_ge(s["exp_done"], i * 2 + half + 1)
                        for u in range(half * NU // 2, (half + 1) * NU // 2):
                            last = nc.tensor.transpose(S[:, u // 4, (u % 4) * P:(u % 4 + 1) * P], e_sb[:, u, :], ident[:, :])
                        last.then_inc(s["pT_ps"], 1)
                    if last_turn:
                        pe.wait_ge(s["w_split"], (e + 1) * PIECES + 2)
                    pe.wait_ge(s["gT_ready"], i + 2)
                    hidden(i + 1, 0)
                    pe.wait_ge(s["pT_low"], i + 2)
                    pe.wait_ge(s["pT_high"], i + 2)
                    pe.wait_ge(s["qk_biased"], i + 2)
                    for u in range(NU):
                        jj, a, g = u // 4, (u // 2) % 2, u % 2
                        last = MM(M[:, u * 32:(u + 1) * 32], pT_sb[:, u, :], (v0, v1)[a][:, g * P + jj * 32:g * P + jj * 32 + 32],
                                  start=True, stop=True)
                    last.then_inc(s["pv_ps"], 1)
                    transpose_qk(i + 1)
                    pe.wait_ge(s["at_ready"], i + 1)
                    project_v(i + 1)
                    hidden(i + 1, 1)
                    pe.wait_ge(s["v_ready"], i + 2)
                    for c in range(DC):
                        last = nc.tensor.transpose(M[:, D + c * P:D + (c + 1) * P], at[:, c * P:(c + 1) * P], ident[:, :])
                    last.then_inc(s["aT_ps"], 1)
                    hidden(i + 1, 2)
                    pe.wait_ge(s["aT_ready"], i + 1)
                    split_product(M[:, 0:D], lambda c: aTh[:, c, :], lambda c: aTl[:, c, :],
                                  lambda c: woh[:, c, :], lambda c: wol[:, c, :], DC).then_inc(s["o_ps"], 1)
                    hidden(i + 1, 3)
                    pe.wait_ge(s["acc_done"], i + 2)
                    transpose_x(i + 2)

                with pe.Fori(0, UE - 1) as j:
                    turn(j, False)
                turn(UE - 1, True)


_INS = ["L0_attn_x", "L0_attn_wq", "L0_attn_bq", "L0_attn_wk", "L0_attn_bk", "L0_attn_wv", "L0_attn_bv", "L0_attn_wo",
        "L0_attn_bo", "L0_attn_qn_w", "L0_attn_kn_w", "L0_ffn_Wr", "L0_ffn_W1", "L0_ffn_W2"]


def kernel(**inputs):
    import numpy as _np
    import concourse.bacc as _bacc
    from concourse import mybir as _mybir
    from concourse.bass_utils import run_bass_kernel_spmd as _run

    nc = _bacc.Bacc("TRN2", target_bir_lowering=False, num_devices=1)
    arrays, args = {}, []
    for name in _INS:
        a = _np.ascontiguousarray(inputs[name])
        arrays[f"in_{name}_dram"] = a
        args.append(nc.dram_tensor(f"in_{name}_dram", a.shape, _mybir.dt.from_np(a.dtype), kind="ExternalInput").ap())
    shape = tuple(inputs["L0_attn_x"].shape)
    args.append(nc.dram_tensor("out_0_dram", shape, _mybir.dt.float32, kind="ExternalOutput").ap())
    attention_and_experts(nc, *args)
    r = _run(nc, [arrays], core_ids=[0])
    return r.results[0]["out_0_dram"]
```

```python
import concourse.bass as bass
from concourse import mybir
from contextlib import ExitStack


P = 128


def attention_and_experts(nc, x, wq, bq, wk, bk, wv, bv, wo, bo, qn_w, kn_w, Wr, W1, W2, out):
    F32, F32R, BF16, I32 = mybir.dt.float32, mybir.dt.float32r, mybir.dt.bfloat16, mybir.dt.int32
    ALU = mybir.AluOpType
    ACT = mybir.ActivationFunctionType
    AX = mybir.AxisListType

    B, T, D = x.shape
    NE, _, FF = W1.shape
    TOPK = 2
    H, WIN = 16, 64
    DH = D // H
    N = B * T
    NT = N // P
    TB = T // P
    DC = D // P
    FCH = FF // P
    ROWS = N * TOPK
    UNIT = ROWS // NT
    US = UNIT // P
    UE = (ROWS // NE) // UNIT
    assert TB == UE and B == NE and WIN * 2 == P
    HP = 4
    NP = H // 2
    NU = HP * 2 * DC
    G4 = 4
    NG = NT // G4
    LN_EPS, RMS_EPS = 1e-5, 1.1920928955078125e-07
    NEG = -1.0e30
    RW = D + 1

    xt = x.rearrange("b t d -> (b t) d").rearrange("(n p) d -> p n d", p=P)
    ot = out.rearrange("b t d -> (b t) d").rearrange("(n p) d -> p n d", p=P)
    routed = nc.dram_tensor("routed_rows", [ROWS + UNIT, RW], F32).ap()
    expert_out = nc.dram_tensor("expert_rows", [ROWS, D], F32).ap()
    routed_t = routed.rearrange("(n p) d -> p n d", p=P)
    expert_t = expert_out.rearrange("(n p k) d -> p n k d", p=P, k=TOPK)
    W1v = W1.rearrange("e (c p) f -> p e c f", p=P)
    W2v = W2.rearrange("e (f p) d -> p e f d", p=P)

    ctx = ExitStack()
    with ctx:
        def sb(name, shape, dt=F32):
            return ctx.enter_context(nc.sbuf_tensor(name, shape, dt))

        def sem(name):
            return ctx.enter_context(nc.semaphore(name))

        xn_all = sb("xn_all", [P, NT + 2, D])
        scratch = sb("scratch", [P, 2 * NU * P + 2 * G4])
        e_sb = scratch[:, 0:NU * P].rearrange("p (u k) -> p u k", k=P)
        pT_sb = scratch[:, NU * P:2 * NU * P].rearrange("p (u k) -> p u k", k=P)
        raw = sb("raw", [P, 2, 1024])
        w1h, w1l = sb("w1h", [P, DC, FF], F32R), sb("w1l", [P, DC, FF], F32R)
        w2h, w2l = sb("w2h", [P, FCH, D], F32R), sb("w2l", [P, FCH, D], F32R)
        wqkvh, wqkvl = sb("wqkvh", [P, DC, 3 * D], F32R), sb("wqkvl", [P, DC, 3 * D], F32R)
        woh, wol = sb("woh", [P, DC, D], F32R), sb("wol", [P, DC, D], F32R)
        masks = sb("masks", [P, 2, 2, P], BF16)
        ident = sb("ident", [P, P])
        identb = sb("identb", [P, P], BF16)
        upper = sb("upper", [P, P], BF16)
        onesb = sb("onesb", [P, P], BF16)
        wrT = sb("wrT", [P, DC, NE])
        qkv_bias = sb("qkv_bias", [P, 3 * D])
        bo_b = sb("bo_b", [P, D])
        nw = sb("nw", [P, 2, DH])
        qw = sb("qw", [P, DH])
        minus_half = sb("minus_half", [P, 1])
        xs = sb("xs", [P, D])
        xTh, xTl = sb("xTh", [P, DC, P], F32R), sb("xTl", [P, DC, P], F32R)
        qkb = sb("qkb", [P, 2 * D])
        sq = sb("sq", [P, 2 * D])[:, :]
        ss = sb("ss", [P, 2 * H])
        rms = sb("rms", [P, 2 * H])
        qT = sb("qT", [P, NP, 2, 2, WIN], F32R)
        kT = sb("kT", [P, NP, WIN + P], F32R)
        v0, v1 = sb("v0", [P, D]), sb("v1", [P, D])
        at = sb("at", [P, D])
        aTh, aTl = sb("aTh", [P, DC, P], F32R), sb("aTl", [P, DC, P], F32R)
        nmax = sb("nmax", [P, NU])
        lsum = sb("lsum", [P, NU])
        rl = sb("rl", [P, NU])
        xres = sb("xres", [P, D])
        xg = sb("xg", [P, US, RW])
        gTh, gTl = sb("gTh", [P, DC, UNIT], F32R), sb("gTl", [P, DC, UNIT], F32R)
        hf = sb("hf", [P, 2, 2 * UNIT])
        pad = hf[:, :, :].rearrange("p s r -> p (s r)")[:, 0:US * RW].rearrange("p (n d) -> p n d", d=RW)
        hh, hl = sb("hh", [P, FCH, UNIT], F32R), sb("hl", [P, FCH, UNIT], F32R)
        ysb = sb("ysb", [P, US, D])
        wr_sb = xres[0:NE, :]
        logits = xg[:, :, :].rearrange("p n d -> p (n d)")[:, 0:NT * NE].rearrange("p (t e) -> p t e", e=NE)
        stats = sb("stats", [P, 2, G4, 6])
        mv = sb("mv", [P, 2, G4, 2])
        rstd = sb("rstd", [P, 2, G4])
        wtop = sb("wtop", [P, TOPK, NT + 2 * G4])
        pidx = sb("pidx", [P, TOPK, NT + 2 * G4], I32)
        place = sb("place", [P, TOPK, NT], I32)
        ist = sb("ist", [P, TOPK, G4], I32)
        next_places = sb("next_places", [P, US], I32)
        places = sb("places", [P, US], I32)
        wst = sb("wst", [P, 4, TOPK, 2])

        flat = scratch[:, :]
        XIN = 4
        xin = flat[:, 0:XIN * G4 * D].rearrange("p (s n d) -> p s n d", s=XIN, d=D)
        xs4 = raw[:, 0, :].rearrange("p (n d) -> p n d", d=D)
        xT4 = raw[:, 1, :].rearrange("p (c t) -> p c t", c=DC)
        logitsT = sq[0:NE, :]

        def arr(k):
            return flat[:, k * 512:(k + 1) * 512]

        qk4 = e_sb[:, :, :].rearrange("p u k -> p (u k)").rearrange("p (s h x y d) -> p s h x y d", s=2, h=H, x=2, y=2)

        xst = flat[:, NU * P:NU * P + TOPK * G4 * RW].rearrange("p (k n d) -> p k n d", k=TOPK, d=RW)
        OUT, GT = 4, 2
        gath = flat[:, 0:OUT * GT * TOPK * D].rearrange("p (s n k d) -> p s n k d", s=OUT, k=TOPK, d=D)
        ost = raw[:, :, :].rearrange("p s (a n d) -> p (s a) n d", a=OUT // 2, d=D)

        S = ctx.enter_context(nc.psum_tensor("scores_ps", [P, HP, 512], F32))
        M = ctx.enter_context(nc.psum_tensor("attn_ps", [P, 512], F32))
        FM = ctx.enter_context(nc.psum_tensor("ffn_ps", [P, 512], F32))
        HB = ctx.enter_context(nc.psum_tensor("hidden_ps", [P, 2, 512], F32))

        names = """pool_held dve_held const_loaded weights_loaded const_made attn_hi attn_split raw_loaded0
            raw_loaded1 w_hi w_split pool_step dve_step xin_loaded0 xin_loaded1 xin_loaded2 xin_loaded3
            stats_ready rstd_ready xs4_ready xn_kept x4_ps x4T_ready logitT_ps logitT_ready logit_ps
            logit_ready wr_ps sel_ready prefix_ps gap_ready gap_exp wtop_ready staged scattered0 scattered1
            pad_ready pad_written xs_ready xT_ps xT_ready qk_ps qk_biased sq_ready ss_ready qw_ready
            qkn_ready v_ps v_ready qk4_hi qk4_ready qkT_ps khalo_ready qkT_even qkT_odd s_ps max_ready
            exp_done pT_ps pT_low pT_high pv_ps at_ready aT_ps aTh_ready aT_ready o_ps acc_done xres_loaded
            xres_ready xg_loaded gT_ps gTh_ready gT_ready h_ps h_evicted h_split y_ps y_evicted y_stored
            places_kept y_free gathered0 gathered1 gathered2 gathered3 combined stored0 stored1 stored2
            stored3""".split()
        s = {n: sem(n) for n in names}
        raw_loaded = [s["raw_loaded0"], s["raw_loaded1"]]
        xin_loaded = [s[f"xin_loaded{k}"] for k in range(XIN)]
        scattered = [s["scattered0"], s["scattered1"]]
        gathered = [s[f"gathered{k}"] for k in range(OUT)]
        stored = [s[f"stored{k}"] for k in range(OUT)]

        PIECES = 4
        N_CONST = 4 + 2 + 1

        def f32(ap):
            return ap.bitcast(F32)

        def w_piece(e, k):
            if k < 2:
                return W1v[:, bass.ds(e, 1), k, :]
            return W2v[:, bass.ds(e, 1), 4 * (k - 2):4 * (k - 1), :]

        def w_part(h1, h2, k):
            if k < 2:
                return h1[:, k, :]
            return h2[:, 4 * (k - 2):4 * (k - 1), :].rearrange("p f d -> p (f d)")

        def start(engine, name, by=1):
            engine.sem_inc(s[name], by)

        block = ctx.enter_context(nc.Block())

        @block.sync
        def _(sp):
            def load(dst, src):
                sp.dma_start(dst, src).then_inc(s["const_loaded"], 16)

            for r in range(OUT):
                start(sp, f"stored{r}", 16)
            for k, w in enumerate((wq, wk, wv, wo)):
                sp.dma_start(raw[:, :, k * D:(k + 1) * D],
                             w.rearrange("(c p) n -> p c n", p=P)).then_inc(s["weights_loaded"], 16)
            for k, b in enumerate((bq, bk, bv)):
                load(qkv_bias[:, k * D:(k + 1) * D], b.rearrange("(o n) -> o n", o=1).to_broadcast([P, D]))
            load(bo_b[:, :], bo.rearrange("(o n) -> o n", o=1).to_broadcast([P, D]))
            for k, w in enumerate((qn_w, kn_w)):
                load(nw[:, k, :], w.rearrange("(o n) -> o n", o=1).to_broadcast([P, DH]))
            load(wr_sb, Wr)

            with sp.Fori(0, NG // XIN) as gx:
                for r in range(XIN):
                    sp.wait_ge(s["xs4_ready"], gx * XIN + r + 1)
                    sp.dma_start(xin[:, r], xt[:, bass.ds(gx * XIN * G4 + r * G4, G4), :]
                                 ).then_inc(xin_loaded[r], 16)

            sp.wait_ge(s["pad_ready"], 1)
            sp.dma_start(routed_t[:, NT * US:(NT + 1) * US, :], pad).then_inc(s["pad_written"], 16)

            def load_piece(e, k):
                sp.dma_start(raw[:, k % 2, :], w_piece(e, k)).then_inc(raw_loaded[k % 2], 16)

            sp.wait_ge(s["logit_ready"], NG + 1)
            load_piece(0, 0)
            load_piece(0, 1)
            for k in range(2, PIECES):
                sp.wait_ge(s["w_split"], k - 1)
                load_piece(0, k)

            for r in range(2):
                sp.wait_ge(scattered[r], 16 * G4 * NG)
            sp.wait_ge(s["pad_written"], 16)
            sp.dma_start(xg[:, :, :], routed_t[:, 0:US, :]).then_inc(s["xg_loaded"], 16)

            with sp.Fori(0, NE) as e:
                def turn(i, last):
                    if last:
                        sp.wait_ge(s["w_split"], (e + 1) * PIECES)
                        for k in range(2):
                            load_piece((e + 1) % NE, k)
                    sp.wait_ge(s["gT_ps"], i + 1)
                    sp.wait_ge(s["places_kept"], i + 1)
                    sp.dma_start(xg[:, :, :], routed_t[:, bass.ds((i + 1) * US, US), :]
                                 ).then_inc(s["xg_loaded"], 16)
                    sp.wait_ge(s["acc_done"], i + 1)
                    sp.dma_start(xres[:, :], xt[:, bass.ds(i, 1), :]).then_inc(s["xres_loaded"], 16)
                    if last:
                        for k in range(2):
                            sp.wait_ge(s["w_split"], (e + 1) * PIECES + k + 1)
                            load_piece((e + 1) % NE, k + 2)

                with sp.Fori(0, UE - 1) as j:
                    turn(e * UE + j, False)
                turn(e * UE + (UE - 1), True)

            sp.wait_ge(s["y_stored"], 16 * US * NT)
            sp.wait_ge(s["acc_done"], NT + 1)
            with sp.Fori(0, NT // GT // OUT) as go:
                for r in range(OUT):
                    sp.wait_ge(s["combined"], go * OUT + r + 1)
                    sp.dma_start(gath[:, r], expert_t[:, bass.ds((go * OUT + r) * GT, GT), :, :]
                                 ).then_inc(gathered[r], 16)
            for r in range(OUT):
                sp.wait_ge(stored[r], 16 * (NT // GT // OUT + 1))
            sp.wait_ge(s["xg_loaded"], 16 * (NT + 1))

        @block.gpsimd
        def _(pool):
            steps = [0]

            def step(ins, base=0):
                steps[0] += 1
                ins.then_inc(s["pool_step"], 1)
                pool.wait_ge(s["pool_step"], base + steps[0])

            def wait(name, value):
                pool.wait_ge(s[name], value)
                pool.sem_inc(s["pool_held"], 1)

            nc.gpsimd.memset(minus_half[:, :], -0.5)
            nc.gpsimd.iota(place[:, :, :], pattern=[[1, TOPK], [TOPK * P, NT]], base=0, channel_multiplier=TOPK)
            nc.gpsimd.memset(onesb[:, :], 1.0)
            nc.gpsimd.memset(upper[:, :], 1.0)
            nc.gpsimd.memset(masks[:, :, :, :], 0.0)
            step(nc.gpsimd.memset(ident[:, :], 0.0))
            step(nc.gpsimd.affine_select(out=ident[:, :], in_=ident[:, :], pattern=[[-1, P]], base=0,
                                         compare_op=ALU.not_equal, fill=1.0, channel_multiplier=1))
            nc.gpsimd.tensor_copy(identb[:, :], ident[:, :])
            nc.gpsimd.affine_select(out=upper[:, :], in_=upper[:, :], pattern=[[1, P]], base=0,
                                    compare_op=ALU.is_gt, fill=0.0, channel_multiplier=-1)
            for h in range(2):
                m = masks[h * WIN:(h + 1) * WIN, :, :, :].rearrange("p j a c -> p (j a) c")
                step(nc.gpsimd.affine_select(out=m, in_=m, pattern=[[0, 4], [1, P]], base=0,
                                             compare_op=ALU.is_gt, fill=NEG, channel_multiplier=-1))
                step(nc.gpsimd.affine_select(out=m, in_=m, pattern=[[0, 4], [-1, P]], base=WIN,
                                             compare_op=ALU.is_ge, fill=NEG, channel_multiplier=1))
                m0 = masks[h * WIN:(h + 1) * WIN, 0, 0, :]
                step(nc.gpsimd.affine_select(out=m0, in_=m0, pattern=[[1, P]], base=-WIN,
                                             compare_op=ALU.is_ge, fill=NEG, channel_multiplier=0))
            nc.gpsimd.memset(xn_all[:, NT:, :], 0.0).then_inc(s["const_made"], 1)

            base0 = steps[0]
            with pool.Fori(0, NG // 2) as g2:
                for r in range(2):
                    g = g2 * 2 + r
                    wait("stats_ready", g + 1)
                    steps[0] = 0
                    step(nc.gpsimd.tensor_scalar(rstd[:, r, :], mv[:, r, :, 1], LN_EPS, None, ALU.add), base0 + g)
                    nc.gpsimd.tensor_tensor(rstd[:, r, :], rstd[:, r, :], minus_half[:, :].to_broadcast([P, G4]),
                                            ALU.pow).then_inc(s["rstd_ready"], 1)
            base0 += NG

            def stage(t):
                if not (isinstance(t, int) and t == 0):
                    wait("xT_ps", t)
                nc.gpsimd.tensor_copy(xs[:, :], xn_all[:, bass.ds(t, 1), :]).then_inc(s["xs_ready"], 1)

            def rms_norm(t, base):
                pool.wait_ge(s["qk_biased"], t + 1)
                nc.gpsimd.tensor_tensor(sq, qkb[:, :], qkb[:, :], ALU.mult).then_inc(s["sq_ready"], 1)
                wait("ss_ready", t + 1)
                step(nc.gpsimd.tensor_scalar(rms[:, :], ss[:, :], 1.0 / DH, RMS_EPS, ALU.mult, ALU.add), base)
                step(nc.gpsimd.tensor_tensor(rms[:, :], rms[:, :], minus_half[:, :].to_broadcast([P, 2 * H]),
                                             ALU.pow), base)
                pool.wait_ge(s["qw_ready"], t + 1)
                q3 = qkb[:, :].rearrange("p (h d) -> p h d", d=DH)
                nc.gpsimd.tensor_tensor(q3, q3, rms[:, :].unsqueeze(2).to_broadcast([P, 2 * H, DH]),
                                        ALU.mult).then_inc(s["qkn_ready"], 1)

            steps[0] = 0
            wait("xn_kept", NG + 1)
            stage(0)
            rms_norm(0, base0)
            base0 += 2

            with pool.Fori(0, NG) as g:
                for k in range(TOPK):
                    wait("staged", g * TOPK + k + 1)
                    for n in range(G4):
                        nc.gpsimd.indirect_dma_start(
                            out=routed[0:ROWS, :], out_offset=bass.IndirectOffsetOnAxis(ap=ist[:, k, n:n + 1], axis=0),
                            in_=xst[:, k, n, :], in_offset=None).then_inc(scattered[k], 16)

            def keep_places(t, base):
                wait("xg_loaded", (t + 1) * 16)
                nc.gpsimd.tensor_copy(next_places[:, :], xg[:, :, D].bitcast(I32)).then_inc(s["places_kept"], 1)

            stage(1)
            keep_places(0, 0)

            def turn(i, base):
                steps[0] = 0
                if not isinstance(i, int):
                    wait("y_stored", i * (16 * US))
                wait("places_kept", i + 1)
                nc.gpsimd.tensor_copy(places[:, :], next_places[:, :]).then_inc(s["y_free"], 1)
                wait("s_ps", i + 1)
                nc.gpsimd.tensor_copy(kT[:, :, 0:WIN], f32(kT[:, :, P:P + WIN])).then_inc(s["khalo_ready"], 1)
                wait("xres_loaded", (i + 1) * 16)
                nc.gpsimd.tensor_tensor(xres[:, :], xres[:, :], bo_b[:, :], ALU.add).then_inc(s["xres_ready"], 1)
                rms_norm(i + 1, base)
                stage(i + 2)
                wait("y_free", i + 1)
                wait("y_evicted", i + 2)
                for n in range(US):
                    nc.gpsimd.indirect_dma_start(
                        out=expert_out[:, :], out_offset=bass.IndirectOffsetOnAxis(ap=places[:, n:n + 1], axis=0),
                        in_=ysb[:, n, :], in_offset=None).then_inc(s["y_stored"], 16)
                keep_places(i + 1, base)

            turn(0, base0)
            with pool.Fori(1, NT) as i:
                turn(i, base0 + i * 2)

        @block.scalar
        def _(act):
            def copy(dst, src, **kw):
                return nc.scalar.activation(dst, src, ACT.Copy, **kw)

            start(act, "h_evicted", 2)
            start(act, "xn_kept")
            act.wait_ge(s["weights_loaded"], 4 * 16)
            for c in range(DC):
                copy(wqkvh[:, c, :], raw[:, c, 0:3 * D])
                copy(woh[:, c, :], raw[:, c, 3 * D:4 * D]).then_inc(s["attn_hi"], 1)
            act.wait_ge(s["wr_ps"], 1)
            copy(wrT[:, :, :], M[:, 0:DC * NE].rearrange("p (c e) -> p c e", e=NE)).then_inc(s["logit_ready"], 1)

            def keep_group(g):
                act.wait_ge(s["xs4_ready"], g + XIN + 1)
                copy(xn_all[:, bass.ds(g * G4, G4), :], xs4).then_inc(s["xn_kept"], 1)

            def keep_transposed(g, r):
                act.wait_ge(s["x4_ps"], g + 2)
                copy(xT4.rearrange("p c t -> p (c t)"),
                     S[:, 2 * r:2 * r + 2, :].rearrange("p b c -> p (b c)")).then_inc(s["x4T_ready"], 1)

            def keep_logitsT(g):
                act.wait_ge(s["logitT_ps"], g + 1)
                copy(logitsT, M[0:NE, :]).then_inc(s["logitT_ready"], 1)

            def keep_logits(g):
                act.wait_ge(s["logit_ps"], g + 1)
                copy(logits[:, bass.ds(g * G4, G4), :], FM[:, :].rearrange("p (n t) -> p n t", t=P)[:, :, 0:NE]
                     ).then_inc(s["logit_ready"], 1)

            keep_group(0)
            keep_transposed(0, 0)
            keep_group(1)
            keep_logitsT(0)
            keep_transposed(1, 1)
            with act.Fori(0, NG // 2 - 1) as g2:
                for r in range(2):
                    keep_group(g2 * 2 + r + 2)
                    keep_logits(g2 * 2 + r)
                    keep_logitsT(g2 * 2 + r + 1)
                    keep_transposed(g2 * 2 + r + 2, r)
            keep_logits(NG - 2)
            keep_logitsT(NG - 1)
            keep_logits(NG - 1)

            act.wait_ge(s["gap_ready"], 1)
            nc.scalar.activation(arr(0)[:, 4 * NT:5 * NT], arr(0)[:, 3 * NT:4 * NT], ACT.Exp).then_inc(s["gap_exp"], 1)

            def parts_hi(t):
                act.wait_ge(s["qkn_ready"], t + 1)
                for k in range(2):
                    src = qkb[:, k * D:(k + 1) * D].rearrange("p (h d) -> p h d", d=DH).unsqueeze(2).to_broadcast([P, H, 2, DH])
                    dst = qk4[:, 0, :, 0, :, :] if k == 0 else qk4[:, 1, :, :, 0, :]
                    copy(dst.bitcast(F32R), src).then_inc(s["qk4_hi"], 1)

            def keep_qk(t):
                for k in range(2):
                    act.wait_ge(s["qkT_ps"], t * 2 + 1 + k)
                    if k == 0:
                        for eo in range(2):
                            h = slice(eo * WIN, (eo + 1) * WIN)
                            copy(qT[h, 0:HP, :, eo, :], S[h, 0, :].rearrange("p (n a w) -> p n a w", a=2, w=WIN))
                    else:
                        if not isinstance(t, int):
                            act.wait_ge(s["khalo_ready"], t)
                        copy(kT[:, 0:HP, WIN:WIN + P], S[:, 2, :].rearrange("p (n k) -> p n k", k=P)
                             ).then_inc(s["qkT_even"], 1)

            def rows_hi(t):
                act.wait_ge(s["gT_ps"], t + 1)
                copy(gTh[:, :, :].rearrange("p c r -> p (c r)"), HB[:, 0, :]).then_inc(s["gTh_ready"], 1)

            def weights_hi(e, k):
                act.wait_ge(raw_loaded[k % 2], (e * 2 + k // 2 + 1) * 16)
                copy(w_part(w1h, w2h, k), raw[:, k % 2, :]).then_inc(s["w_hi"], 1)

            def gelu(u, q):
                act.wait_ge(s["h_ps"], u * 4 + q + 1)
                act.wait_ge(s["h_split"], u * 4 + q + 1)
                nc.scalar.activation(hf[:, q % 2, :], HB[:, q % 2, :], ACT.Gelu)
                nc.scalar.activation(hh[:, 2 * q:2 * q + 2, :], HB[:, q % 2, :].rearrange("p (n r) -> p n r", n=2),
                                     ACT.Gelu).then_inc(s["h_evicted"], 1)

            for k in range(PIECES):
                weights_hi(0, k)
            act.wait_ge(s["wtop_ready"], 1)
            parts_hi(0)
            keep_qk(0)
            rows_hi(0)
            for q in range(4):
                gelu(0, q)
            with act.Fori(0, NE) as e:
                def turn(i, last):
                    if last:
                        weights_hi(e + 1, 0)
                        weights_hi(e + 1, 1)
                    rows_hi(i + 1)
                    act.wait_ge(s["max_ready"], i + 1)
                    for u in range(NU):
                        jj, ag = u // 4, u % 4
                        ex = nc.scalar.activation(e_sb[:, u, :], S[:, jj, ag * P:(ag + 1) * P], ACT.Exp,
                                                  bias=nmax[:, u:u + 1], accum_out=lsum[:, u:u + 1])
                        if u % (NU // 2) == NU // 2 - 1:
                            ex.then_inc(s["exp_done"], 1)
                    act.wait_ge(s["pT_ps"], i * 2 + 2)
                    copy(pT_sb[:, NU // 2:, :].rearrange("p u k -> p (u k)"), S[:, 2:4, :].rearrange("p b c -> p (b c)")
                         ).then_inc(s["pT_high"], 1)
                    gelu(i + 1, 0)
                    parts_hi(i + 1)
                    gelu(i + 1, 1)
                    if last:
                        act.wait_ge(s["y_ps"], i + 1)
                        weights_hi(e + 1, 2)
                        weights_hi(e + 1, 3)
                    act.wait_ge(s["aT_ps"], i + 1)
                    copy(aTh[:, :, :].rearrange("p c t -> p (c t)"), M[:, D:2 * D]).then_inc(s["aTh_ready"], 1)
                    gelu(i + 1, 2)
                    keep_qk(i + 1)
                    gelu(i + 1, 3)

                with act.Fori(0, UE - 1) as j:
                    turn(e * UE + j, False)
                turn(e * UE + (UE - 1), True)

            with act.Fori(0, NT // GT // OUT) as go:
                for r in range(OUT):
                    act.wait_ge(s["combined"], go * OUT + r + OUT + 1)
                    nc.scalar.dma_start(ot[:, bass.ds((go * OUT + r) * GT, GT), :], ost[:, r]).then_inc(stored[r], 16)

        @block.vector
        def _(dve):
            V = nc.vector
            steps = [0]

            def step(ins, base=0):
                steps[0] += 1
                ins.then_inc(s["dve_step"], 1)
                dve.wait_ge(s["dve_step"], base + steps[0])

            start(dve, "xs4_ready", XIN)
            start(dve, "h_split", 2)
            start(dve, "acc_done")
            start(dve, "y_evicted")
            V.memset(v1[:, :], 0.0)
            V.memset(sq, 0.0)
            V.memset(pidx[:, :, NT:], 0)
            V.memset(wtop[:, :, NT:], 0.0)
            V.memset(pad[:, :, :], 0.0).then_inc(s["pad_ready"], 1)

            for c in range(DC):
                dve.wait_ge(s["attn_hi"], c + 1)
                V.tensor_tensor(wqkvl[:, c, :], raw[:, c, 0:3 * D], f32(wqkvh[:, c, :]), ALU.subtract)
                V.tensor_tensor(wol[:, c, :], raw[:, c, 3 * D:4 * D], f32(woh[:, c, :]),
                                ALU.subtract).then_inc(s["attn_split"], 1)

            dve.wait_ge(s["const_made"], 1)
            dve.wait_ge(s["const_loaded"], 16 * N_CONST)
            step(V.tensor_tensor(qw[:, :], nw[:, 0, :], nw[:, 1, :], ALU.mult))
            step(V.tensor_scalar(qw[:, :], qw[:, :], DH ** -0.5, None, ALU.mult))

            def statistics(g, x, loads):
                r = x % 2
                dve.wait_ge(xin_loaded[x], loads * 16)
                for n in range(G4):
                    last = V.bn_stats(stats[:, r, n, :], xin[:, x, n, :])
                last.then_inc(s["dve_step"], 1)
                dve.wait_ge(s["dve_step"], g + (2 + 1))
                dve.sem_inc(s["dve_held"], 1)
                for n in range(G4):
                    last = V.bn_aggr(mv[:, r, n, :], stats[:, r, n, :])
                last.then_inc(s["stats_ready"], 1)

            def normalise(g, x):
                r = x % 2
                dve.wait_ge(s["rstd_ready"], g + 1)
                dve.wait_ge(s["xn_kept"], g + 1)
                dve.wait_ge(s["x4_ps"], g + 1)
                for n in range(G4):
                    last = V.tensor_scalar(xs4[:, n, :], xin[:, x, n, :], mv[:, r, n, 0:1], rstd[:, r, n:n + 1],
                                           ALU.subtract, ALU.mult)
                last.then_inc(s["xs4_ready"], 1)

            dve.wait_ge(s["attn_split"], 2)
            statistics(0, 0, 1)
            with dve.Fori(0, NG // XIN - 1) as gx:
                for x in range(XIN):
                    statistics(gx * XIN + x + 1, (x + 1) % XIN, gx + 1 + (x + 1) // XIN)
                    normalise(gx * XIN + x, x)
            for x in range(XIN):
                if x < XIN - 1:
                    statistics(NG - XIN + x + 1, x + 1, NG // XIN)
                normalise(NG - XIN + x, x)
            base = 2 + NG

            def hi_lo_x(t):
                dve.wait_ge(s["xT_ps"], t + 1)
                ps = FM[:, 0:D].rearrange("p (c k) -> p c k", k=P)
                step(V.tensor_copy(xTh[:, :, :], ps), cur[0])
                V.tensor_tensor(xTl[:, :, :], ps, f32(xTh[:, :, :]), ALU.subtract).then_inc(s["xT_ready"], 1)

            def bias_qk(t):
                dve.wait_ge(s["qk_ps"], t + 1)
                V.tensor_tensor(qkb[:, :], M[:, :], qkv_bias[:, 0:2 * D], ALU.add).then_inc(s["qk_biased"], 1)

            def square_sums(t):
                dve.wait_ge(s["sq_ready"], t + 1)
                V.tensor_reduce(ss[:, :], sq.rearrange("p (h d) -> p h d", d=DH), AX.X,
                                ALU.add).then_inc(s["ss_ready"], 1)
                q3 = qkb[:, 0:D].rearrange("p (h d) -> p h d", d=DH)
                V.tensor_tensor(q3, q3, qw[:, :].unsqueeze(1).to_broadcast([P, H, DH]), ALU.mult).then_inc(s["qw_ready"], 1)

            def parts_lo(t):
                for k in range(2):
                    dve.wait_ge(s["qk4_hi"], t * 2 + k + 1)
                    src = qkb[:, k * D:(k + 1) * D].rearrange("p (h d) -> p h d", d=DH).unsqueeze(2).to_broadcast([P, H, 2, DH])
                    hi = qk4[:, 0, :, 0, :, :] if k == 0 else qk4[:, 1, :, :, 0, :]
                    lo = qk4[:, 0, :, 1, :, :] if k == 0 else qk4[:, 1, :, :, 1, :]
                    V.tensor_tensor(lo.bitcast(F32R), src, hi, ALU.subtract).then_inc(s["qk4_ready"], 1)

            def keep_q(t):
                dve.wait_ge(s["qkT_ps"], t * 2 + 1)
                for eo in range(2):
                    h = slice(eo * WIN, (eo + 1) * WIN)
                    V.tensor_copy(qT[h, HP:NP, :, eo, :], S[h, 1, :].rearrange("p (n a w) -> p n a w", a=2, w=WIN))

            def keep_k(t):
                dve.wait_ge(s["qkT_ps"], t * 2 + 2)
                if not isinstance(t, int):
                    dve.wait_ge(s["khalo_ready"], t)
                V.tensor_copy(kT[:, HP:NP, WIN:WIN + P], S[:, 3, :].rearrange("p (n k) -> p n k", k=P)
                              ).then_inc(s["qkT_odd"], 1)

            def values(t):
                bv_b = qkv_bias[:, 2 * D:3 * D]
                step(V.tensor_copy(v0[0:WIN, :], v1[WIN:P, :]), cur[0])
                dve.wait_ge(s["v_ps"], t + 1)
                V.tensor_tensor(v0[WIN:P, :], M[0:WIN, 0:D], bv_b[0:WIN, :], ALU.add)
                V.tensor_tensor(v1[:, :], M[:, 0:D], bv_b, ALU.add).then_inc(s["v_ready"], 1)

            def rows_lo(t):
                dve.wait_ge(s["gTh_ready"], t + 1)
                V.tensor_tensor(gTl[:, :, :].rearrange("p c r -> p (c r)"), HB[:, 0, :],
                                f32(gTh[:, :, :].rearrange("p c r -> p (c r)")), ALU.subtract).then_inc(s["gT_ready"], 1)

            def weights_lo(e, k):
                dve.wait_ge(s["w_hi"], e * PIECES + k + 1)
                V.tensor_tensor(w_part(w1l, w2l, k), raw[:, k % 2, :], f32(w_part(w1h, w2h, k)),
                                ALU.subtract).then_inc(s["w_split"], 1)

            def split(u, q):
                dve.wait_ge(s["h_evicted"], u * 4 + q + 3)
                V.tensor_tensor(hl[:, 2 * q:2 * q + 2, :], hf[:, q % 2, :].rearrange("p (n r) -> p n r", n=2),
                                f32(hh[:, 2 * q:2 * q + 2, :]), ALU.subtract).then_inc(s["h_split"], 1)

            steps[0] = 0
            cur = [base]
            hi_lo_x(0)

            dve.wait_ge(s["logit_ready"], NG + 1)
            dve.wait_ge(s["xn_kept"], NG + 1)
            L = logits
            rank = arr(0).rearrange("p (n e) -> p n e", e=NE)
            tmp = arr(1).rearrange("p (n e) -> p n e", e=NE)
            top = [arr(2).rearrange("p (n e) -> p n e", e=NE), arr(3).rearrange("p (n e) -> p n e", e=NE)]
            for o in range(NE):
                first = V.memset(rank[:, :, o:o + 1], float(NE - 1 - o))
            step(first, base)
            for d in range(1, NE):
                wins = tmp[:, :, 0:NE - d]
                step(V.tensor_tensor(wins, L[:, :, 0:NE - d], L[:, :, d:NE], ALU.is_ge), base)
                step(V.tensor_tensor(rank[:, :, 0:NE - d], rank[:, :, 0:NE - d], wins, ALU.subtract), base)
                step(V.tensor_tensor(rank[:, :, d:NE], rank[:, :, d:NE], wins, ALU.add), base)
                if d == 2:
                    bias_qk(0)
                if d == 5:
                    square_sums(0)
            for k in range(TOPK):
                step(V.tensor_scalar(top[k], rank, float(k), None, ALU.is_equal), base)
            sel = arr(4)[:, 0:256].bitcast(BF16).rearrange("p (e n) -> p e n", e=NE)
            V.tensor_scalar(sel.rearrange("p e n -> p n e"), rank, float(TOPK) - 0.5, None,
                            ALU.is_lt).then_inc(s["sel_ready"], 1)
            dve.wait_ge(s["prefix_ps"], 1)
            ones512 = arr(0)
            step(V.memset(ones512, 1.0), base)
            step(V.tensor_tensor_scan(arr(7), ones512, S[:, 1, :], 0.0, ALU.mult, ALU.add), base)
            step(V.tensor_tensor(arr(7), arr(7), S[:, 1, :], ALU.subtract), base)
            step(V.tensor_tensor(arr(7), arr(7), S[:, 0, :], ALU.add), base)
            pos = arr(7).rearrange("p (e n) -> p n e", e=NE)

            def stage_rows(g, k):
                V.tensor_copy(ist[:, k, :], pidx[:, k, bass.ds(g * G4, G4)])
                V.tensor_copy(xst[:, k, :, D].bitcast(I32), place[:, k, bass.ds(g * G4, G4)])
                V.tensor_copy(xst[:, k, :, 0:D], xn_all[:, bass.ds(g * G4, G4), :]).then_inc(s["staged"], 1)

            def choice(k, src, dst):
                step(V.tensor_tensor(tmp, top[k], src, ALU.mult), base)
                step(V.tensor_reduce(dst, tmp, AX.X, ALU.add), base)

            ptop, l0, l1, gap, gap_e, total = [arr(0)[:, NT * k:NT * (k + 1)] for k in range(6)]
            for k in range(TOPK):
                choice(k, pos, ptop)
                step(V.tensor_copy(pidx[:, k, 0:NT], ptop), base)
                stage_rows(0, k)
            choice(0, L, l0)
            choice(1, L, l1)
            V.tensor_tensor(gap, l1, l0, ALU.subtract).then_inc(s["gap_ready"], 1)
            dve.wait_ge(s["gap_exp"], 1)
            step(V.tensor_scalar(total, gap_e, 1.0, None, ALU.add), base)
            step(V.reciprocal(wtop[:, 0, 0:NT], total), base)
            V.tensor_tensor(wtop[:, 1, 0:NT], wtop[:, 0, 0:NT], gap_e, ALU.mult).then_inc(s["wtop_ready"], 1)

            def stage_group(g):
                for k in range(TOPK):
                    dve.wait_ge(scattered[k], g * (16 * G4))
                    stage_rows(g, k)

            stage_group(1)
            V.memset(f32(kT[:, :, :]), 0.0)
            step(V.memset(f32(qT[:, :, :, :, :]), 0.0), base)
            weights_lo(0, 0)
            weights_lo(0, 1)
            stage_group(2)
            weights_lo(0, 2)
            weights_lo(0, 3)
            stage_group(3)
            values(0)
            parts_lo(0)
            stage_group(4)
            keep_q(0)
            keep_k(0)
            with dve.Fori(5, NG) as g:
                stage_group(g)
            rows_lo(0)
            for q in range(4):
                split(0, q)
            hi_lo_x(1)
            base += steps[0]
            PER = 1 + 1 + 1
            with dve.Fori(0, NE) as e:
                def turn(i, last):
                    cur[0] = i * PER + base
                    steps[0] = 0
                    dve.wait_ge(s["s_ps"], i + 1)
                    V.tensor_reduce(nmax[:, :], S[:, :, :].rearrange("p j (u k) -> p (j u) k", k=P), AX.X, ALU.max,
                                    negate=True).then_inc(s["max_ready"], 1)
                    bias_qk(i + 1)
                    if last:
                        weights_lo(e + 1, 0)
                        weights_lo(e + 1, 1)
                    rows_lo(i + 1)
                    square_sums(i + 1)
                    dve.wait_ge(s["y_ps"], i + 1)
                    dve.wait_ge(s["y_free"], i + 1)
                    V.tensor_copy(ysb[:, :, :].rearrange("p n d -> p (n d)"), FM[:, :]).then_inc(s["y_evicted"], 1)
                    dve.wait_ge(s["pT_ps"], i * 2 + 1)
                    V.tensor_copy(pT_sb[:, 0:NU // 2, :].rearrange("p u k -> p (u k)"),
                                  S[:, 0:2, :].rearrange("p b c -> p (b c)")).then_inc(s["pT_low"], 1)
                    dve.wait_ge(s["exp_done"], i * 2 + 2)
                    step(V.reciprocal(rl[:, :], lsum[:, :]), cur[0])
                    split(i + 1, 0)
                    parts_lo(i + 1)
                    dve.wait_ge(s["pv_ps"], i + 1)
                    for a in range(2):
                        for eo in range(2):
                            q = slice(eo * WIN, (eo + 1) * WIN)
                            src = M[q, :].rearrange("p (j a g e d) -> p j a g e d", j=HP, a=2, g=DC, e=2)[:, :, a, :, eo, :]
                            inv = rl[q, :].rearrange("p (j a g) -> p j a g", j=HP, a=2)[:, :, a, :]
                            dst = at[a * WIN:(a + 1) * WIN, :].rearrange("p (g j e d) -> p j g e d", g=DC, j=HP, e=2)[:, :, :, eo, :]
                            out_h = V.tensor_tensor(dst, src, inv.unsqueeze(3).to_broadcast([WIN, HP, DC, DH]), ALU.mult)
                    out_h.then_inc(s["at_ready"], 1)
                    split(i + 1, 1)
                    dve.wait_ge(s["aTh_ready"], i + 1)
                    V.tensor_tensor(aTl[:, :, :].rearrange("p c t -> p (c t)"), M[:, D:2 * D],
                                    f32(aTh[:, :, :].rearrange("p c t -> p (c t)")), ALU.subtract).then_inc(s["aT_ready"], 1)
                    keep_q(i + 1)
                    dve.wait_ge(s["o_ps"], i + 1)
                    dve.wait_ge(s["xres_ready"], i + 1)
                    V.tensor_tensor(xn_all[:, bass.ds(i, 1), :], M[:, 0:D].unsqueeze(1), xres[:, :].unsqueeze(1),
                                    ALU.add).then_inc(s["acc_done"], 1)
                    keep_k(i + 1)
                    split(i + 1, 2)
                    values(i + 1)
                    hi_lo_x(i + 2)
                    if last:
                        weights_lo(e + 1, 2)
                        weights_lo(e + 1, 3)
                    split(i + 1, 3)
                    assert steps[0] == PER

                with dve.Fori(0, UE - 1) as j:
                    turn(e * UE + j, False)
                turn(e * UE + (UE - 1), True)
            base += PER * NT

            def stage_weights(g, r):
                V.tensor_copy(wst[:, r, :, :], wtop[:, :, bass.ds(g * GT, GT)]).then_inc(s["combined"], 1)

            for r in range(2):
                dve.wait_ge(raw_loaded[r], 16 * 2 * (NE + 1))
            for r in range(OUT):
                stage_weights(r, r)
            with dve.Fori(0, NT // GT // OUT) as go:
                for r in range(OUT):
                    g = go * OUT + r
                    dve.wait_ge(gathered[r], (go + 1) * 16)
                    dve.wait_ge(s["combined"], g + 1)
                    dve.wait_ge(stored[r], (go + 1) * 16)
                    for n in range(GT):
                        last = V.scalar_tensor_tensor(ost[:, r, n:n + 1, :], gath[:, r, n, 0:1, :], wst[:, r, 0, n:n + 1],
                                                      xn_all[:, bass.ds(g * GT + n, 1), :], ALU.mult, ALU.add)
                    last.then_inc(s["dve_step"], 1)
                    dve.wait_ge(s["dve_step"], g * 2 + (base + 1))
                    for n in range(GT):
                        last = V.scalar_tensor_tensor(ost[:, r, n, :], gath[:, r, n, 1, :], wst[:, r, 1, n:n + 1],
                                                      ost[:, r, n, :], ALU.mult, ALU.add)
                    last.then_inc(s["dve_step"], 1)
                    dve.wait_ge(s["dve_step"], g * 2 + (base + 2))
                    stage_weights(g + OUT, r)

        @block.tensor
        def _(pe):
            MM = nc.tensor.matmul

            def split_product(dst, ah, al, bh, bl, n, start=True, stop=True):
                for c in range(n):
                    for k, (a, b) in enumerate(((ah, bh), (al, bh), (ah, bl))):
                        last = MM(dst, a(c), b(c), start=(start and c == 0 and k == 0), stop=(stop and c == n - 1 and k == 2))
                return last

            start(pe, "x4_ps")
            pe.wait_ge(s["const_made"], 1)
            pe.wait_ge(s["const_loaded"], 16 * N_CONST)
            for c in range(DC):
                last = nc.tensor.transpose(M[:, c * NE:(c + 1) * NE], wr_sb[:, c * P:(c + 1) * P], ident[0:NE, 0:NE])
            last.then_inc(s["wr_ps"], 1)

            def transpose_group(g, r):
                pe.wait_ge(s["xs4_ready"], g + XIN + 1)
                for n in range(G4):
                    for c in range(DC):
                        last = nc.tensor.transpose(S[:, 2 * r + c, n * P:(n + 1) * P],
                                                   xs4[:, n, c * P:(c + 1) * P], ident[:, :])
                last.then_inc(s["x4_ps"], 1)

            def router(g):
                pe.wait_ge(s["x4T_ready"], g + 1)
                for c in range(DC):
                    last = MM(M[0:NE, :], wrT[:, c, :], xT4[:, c, :], start=(c == 0), stop=(c == DC - 1))
                last.then_inc(s["logitT_ps"], 1)

            def back(g):
                pe.wait_ge(s["logitT_ready"], g + 1)
                pe.wait_ge(s["logit_ready"], g + 1)
                for n in range(G4):
                    last = nc.tensor.transpose(FM[:, n * P:(n + 1) * P], sq[:, n * P:(n + 1) * P], ident[:, :])
                last.then_inc(s["logit_ps"], 1)

            transpose_group(0, 0)
            transpose_group(1, 1)
            pe.wait_ge(s["logit_ready"], 1)
            router(0)
            with pe.Fori(0, NG // 2 - 1) as g2:
                for r in range(2):
                    transpose_group(g2 * 2 + r + 2, r)
                    back(g2 * 2 + r)
                    router(g2 * 2 + r + 1)
            back(NG - 2)
            router(NG - 1)
            back(NG - 1)

            def transpose_x(t):
                pe.wait_ge(s["xs_ready"], t + 1)
                for c in range(DC):
                    last = nc.tensor.transpose(FM[:, c * P:(c + 1) * P], xs[:, c * P:(c + 1) * P], ident[:, :])
                last.then_inc(s["xT_ps"], 1)

            pe.wait_ge(s["logit_ready"], NG + 1)
            def project_qk(t):
                pe.wait_ge(s["xT_ready"], t + 1)
                split_product(M[:, :], lambda c: xTh[:, c, :], lambda c: xTl[:, c, :],
                              lambda c: wqkvh[:, c, 0:2 * D], lambda c: wqkvl[:, c, 0:2 * D], DC).then_inc(s["qk_ps"], 1)

            transpose_x(0)
            pe.wait_ge(s["attn_split"], 2)
            project_qk(0)

            pe.wait_ge(s["sel_ready"], 1)
            sel = arr(4)[:, 0:256].bitcast(BF16)
            MM(S[:, 0, :], upper[:, :], sel, start=True, stop=True)
            MM(S[:, 1, :], onesb[:, :], sel, start=True, stop=True).then_inc(s["prefix_ps"], 1)

            def project_v(t):
                split_product(M[:, 0:D], lambda c: xTh[:, c, :], lambda c: xTl[:, c, :],
                              lambda c: wqkvh[:, c, 2 * D:3 * D], lambda c: wqkvl[:, c, 2 * D:3 * D], DC).then_inc(s["v_ps"], 1)

            def transpose_rows(t):
                pe.wait_ge(s["xg_loaded"], (t + 1) * 16)
                if not isinstance(t, int):
                    pe.wait_ge(s["h_evicted"], t * 4 + 1)
                for c in range(DC):
                    for n in range(US):
                        k = c * US + n
                        last = nc.tensor.transpose(HB[:, 0, k * P:(k + 1) * P], xg[:, n, c * P:(c + 1) * P], ident[:, :])
                last.then_inc(s["gT_ps"], 1)

            def transpose_qk(t):
                for k in range(2):
                    pe.wait_ge(s["qk4_ready"], t * 2 + k + 1)
                    for n in range(NP):
                        last = nc.tensor.transpose(S[:, 2 * k + n // HP, (n % HP) * P:(n % HP + 1) * P],
                                                   e_sb[:, k * NP + n, :], ident[:, :])
                    last.then_inc(s["qkT_ps"], 1)

            HIDDEN = 2 * DC * 3

            def hidden_product(q, n):
                f, c, k = 2 * q + n // (DC * 3), n // 3 % DC, n % 3
                return MM(HB[:, q % 2, (f % 2) * UNIT:(f % 2 + 1) * UNIT],
                          (w1h, w1l, w1h)[k][:, c, f * P:(f + 1) * P], (gTh, gTh, gTl)[k][:, c, :],
                          start=(c == 0 and k == 0), stop=(c == DC - 1 and k == 2))

            def hidden(u, q, n0=0, n1=HIDDEN):
                if n0 == 0:
                    pe.wait_ge(s["h_evicted"], u * 4 + q + 1)
                for n in range(n0, n1):
                    last = hidden_product(q, n)
                if n1 == HIDDEN:
                    last.then_inc(s["h_ps"], 1)

            def expert(n):
                return split_product(FM[:, n * D:(n + 1) * D],
                                     lambda c: hh[:, c, n * P:(n + 1) * P], lambda c: hl[:, c, n * P:(n + 1) * P],
                                     lambda c: w2h[:, c, :], lambda c: w2l[:, c, :], FCH)

            pe.wait_ge(s["qk_biased"], 1)
            project_v(0)
            transpose_qk(0)
            transpose_rows(0)
            pe.wait_ge(s["w_split"], 2)
            pe.wait_ge(s["gT_ready"], 1)
            for q in range(4):
                hidden(0, q)
            transpose_x(1)

            with pe.Fori(0, NE) as e:
                def turn(j, last_turn):
                    i = e * UE + j
                    pe.wait_ge(s["qkT_even"], i + 1)
                    pe.wait_ge(s["qkT_odd"], i + 1)
                    for jj in range(HP):
                        kind = 0 if isinstance(j, int) and j == 0 else 1
                        MM(S[:, jj, :], identb[:, :], masks[:, kind, :, :].unsqueeze(2).to_broadcast([P, 2, DC, P]),
                           start=True, stop=False)
                    for a in range(2):
                        for g in range(DC):
                            for jj in range(HP):
                                ag = a * DC + g
                                last = MM(S[:, jj, ag * P:(ag + 1) * P],
                                          qT[:, g * HP + jj, a, :, :].rearrange("p e w -> p (e w)"),
                                          kT[:, g * HP + jj, a * WIN:a * WIN + P], start=False, stop=(ag == 3))
                    last.then_inc(s["s_ps"], 1)
                    pe.wait_ge(s["v_ready"], i + 1)
                    project_qk(i + 1)
                    transpose_rows(i + 1)
                    pe.wait_ge(s["h_split"], i * 4 + 6)
                    pe.wait_ge(s["w_split"], e * PIECES + 4)
                    pe.wait_ge(s["y_evicted"], i + 1)
                    expert(0)
                    expert(1).then_inc(s["y_ps"], 1)
                    def transpose_exp(half):
                        pe.wait_ge(s["exp_done"], i * 2 + half + 1)
                        for u in range(half * NU // 2, (half + 1) * NU // 2):
                            last = nc.tensor.transpose(S[:, u // 4, (u % 4) * P:(u % 4 + 1) * P], e_sb[:, u, :], ident[:, :])
                        last.then_inc(s["pT_ps"], 1)

                    transpose_exp(0)
                    if last_turn:
                        pe.wait_ge(s["w_split"], (e + 1) * PIECES + 2)
                    pe.wait_ge(s["gT_ready"], i + 2)
                    hidden(i + 1, 0)
                    transpose_exp(1)
                    pe.wait_ge(s["qk_biased"], i + 2)
                    pe.wait_ge(s["h_evicted"], (i + 1) * 4 + 2)
                    for half in range(2):
                        pe.wait_ge(s[("pT_low", "pT_high")[half]], i + 1)
                        for u in range(half * NU // 2, (half + 1) * NU // 2):
                            jj, a, g = u // 4, (u // 2) % 2, u % 2
                            cols = slice(g * P + jj * 32, g * P + jj * 32 + 32)
                            if u % 4 != 3:
                                hid = hidden_product(1, u - u // 4)
                            last = MM(M[:, u * 32:(u + 1) * 32], pT_sb[:, u, :], (v0, v1)[a][:, cols], start=True, stop=True)
                            if u == NU - 2:
                                hid.then_inc(s["h_ps"], 1)
                    last.then_inc(s["pv_ps"], 1)
                    hidden(i + 1, 2)
                    pe.wait_ge(s["y_evicted"], i + 2)
                    transpose_x(i + 2)
                    pe.wait_ge(s["at_ready"], i + 1)
                    for c in range(DC):
                        last = nc.tensor.transpose(M[:, D + c * P:D + (c + 1) * P], at[:, c * P:(c + 1) * P], ident[:, :])
                    last.then_inc(s["aT_ps"], 1)
                    transpose_qk(i + 1)
                    pe.wait_ge(s["aT_ready"], i + 1)
                    split_product(M[:, 0:D], lambda c: aTh[:, c, :], lambda c: aTl[:, c, :],
                                  lambda c: woh[:, c, :], lambda c: wol[:, c, :], DC).then_inc(s["o_ps"], 1)
                    hidden(i + 1, 3, 0, HIDDEN * 3 // 4)
                    pe.wait_ge(s["acc_done"], i + 2)
                    project_v(i + 1)
                    hidden(i + 1, 3, HIDDEN * 3 // 4, HIDDEN)

                turn(0, False)
                with pe.Fori(1, UE - 1) as j:
                    turn(j, False)
                turn(UE - 1, True)


_INS = ["L0_attn_x", "L0_attn_wq", "L0_attn_bq", "L0_attn_wk", "L0_attn_bk", "L0_attn_wv", "L0_attn_bv", "L0_attn_wo",
        "L0_attn_bo", "L0_attn_qn_w", "L0_attn_kn_w", "L0_ffn_Wr", "L0_ffn_W1", "L0_ffn_W2"]


def kernel(**inputs):
    import numpy as _np
    import concourse.bacc as _bacc
    from concourse import mybir as _mybir
    from concourse.bass_utils import run_bass_kernel_spmd as _run

    nc = _bacc.Bacc("TRN2", target_bir_lowering=False, num_devices=1)
    arrays, args = {}, []
    for name in _INS:
        a = _np.ascontiguousarray(inputs[name])
        arrays[f"in_{name}_dram"] = a
        args.append(nc.dram_tensor(f"in_{name}_dram", a.shape, _mybir.dt.from_np(a.dtype), kind="ExternalInput").ap())
    shape = tuple(inputs["L0_attn_x"].shape)
    args.append(nc.dram_tensor("out_0_dram", shape, _mybir.dt.float32, kind="ExternalOutput").ap())
    attention_and_experts(nc, *args)
    r = _run(nc, [arrays], core_ids=[0])
    return r.results[0]["out_0_dram"]
```
